# Optimizing a Trainium2 kernel written in Bass

```python
import numpy as np
import jax
import jax.numpy as jnp

def _softmax(x, axis=-1):
    return jax.nn.softmax(x, axis=axis)

def _gelu(x):
    return jax.nn.gelu(x, approximate=True)

def _silu(x):
    return jax.nn.silu(x)

def _sigmoid(x):
    return jax.nn.sigmoid(x)

def _layernorm(x, axis=-1, eps=1e-05):
    m = jnp.mean(x, axis=axis, keepdims=True)
    v = jnp.var(x, axis=axis, keepdims=True)
    return (x - m) / jnp.sqrt(v + eps)

def _scatter_add(tgt, idx, src, axis=0):
    return tgt.at[idx].add(src)

def _segment_sum(src, seg, n):
    return jax.ops.segment_sum(src, seg, n)
kernel_name = 'mk_cond_seq_d1_seqx_r4_6297ac'

def setup_inputs(seed: int=0):
    np.random.seed(seed)
    _w = jnp.asarray

    def _rec_inputs():
        import jax
        import jax.numpy as jnp
        _rk = jax.random.key(seed)
        x = -0.0003929 + 0.9999 * jax.random.normal(jax.random.fold_in(_rk, 1), (16, 256, 256), jnp.float32)
        _lenS = 256 - jax.random.randint(jax.random.fold_in(_rk, 7), (16,), 0, max(1, 256 // 4) + 1, jnp.int32)
        _lenS2 = 256 - jax.random.randint(jax.random.fold_in(_rk, 8), (16,), 0, max(1, 256 // 4) + 1, jnp.int32)
        cond_1024 = 0.00782532 + 1.00527 * jax.random.normal(jax.random.fold_in(_rk, 11), (16, 256), jnp.float32)
        return (x, cond_1024)
    x, cond_1024 = _rec_inputs()

    def _L0_cond_setup():
        import jax, jax.numpy as jnp
        import numpy as np
        B, L, D, P = (8, 512, 256, 64)

        def _ln(x):
            m = x.mean(-1, keepdims=True)
            v = x.var(-1, keepdims=True)
            return (x - m) * jax.lax.rsqrt(v + 1e-05)

        def _s5(u, Lam_re, Lam_im, B_re, B_im, C_re, C_im, D_diag, log_step):
            Lam = Lam_re + 1j * Lam_im
            dt = jnp.exp(log_step)
            Lam_bar = jnp.exp(Lam * dt)
            Bc = B_re + 1j * B_im
            B_bar = ((Lam_bar - 1.0) / Lam)[:, None] * Bc
            Bu = jnp.einsum('bld,pd->blp', u.astype(B_bar.dtype), B_bar)
            A = jnp.broadcast_to(Lam_bar, Bu.shape)

            def binop(e1, e2):
                a1, b1 = e1
                a2, b2 = e2
                return (a1 * a2, a2 * b1 + b2)
            _, xs = jax.lax.associative_scan(binop, (A, Bu), axis=1)
            Cc = C_re + 1j * C_im
            return 2.0 * jnp.einsum('blp,dp->bld', xs, Cc).real + D_diag * u
        key = jax.random.key(seed)
        ks = jax.random.split(key, 16)
        inp = {'y': jax.random.normal(ks[0], (B, L, D), jnp.float32), 't': jax.random.normal(ks[1], (B, D), jnp.float32), 'Wm': jax.random.normal(ks[2], (D, 6 * D), jnp.float32) * 0.02, 'bm': jax.random.normal(ks[3], (6 * D,), jnp.float32) * 0.02, 'Lam_re': -0.5 * jnp.ones((P,), jnp.float32), 'Lam_im': jnp.pi * jnp.arange(P, dtype=jnp.float32), 'B_re': jax.random.normal(ks[4], (P, D), jnp.float32) / np.sqrt(D), 'B_im': jax.random.normal(ks[5], (P, D), jnp.float32) / np.sqrt(D), 'C_re': jax.random.normal(ks[6], (D, P), jnp.float32) / np.sqrt(P), 'C_im': jax.random.normal(ks[7], (D, P), jnp.float32) / np.sqrt(P), 'D_diag': jax.random.normal(ks[8], (D,), jnp.float32), 'log_step': jax.random.uniform(ks[9], (P,), jnp.float32, np.log(0.001), np.log(0.1)), 'Wc': jax.random.normal(ks[10], (D, 2 * D), jnp.float32) * 0.02, 'bc': jax.random.normal(ks[11], (2 * D,), jnp.float32) * 0.02, 'W1': jax.random.normal(ks[12], (D, 4 * D), jnp.float32) / np.sqrt(D), 'b1': jnp.zeros((4 * D,), jnp.float32), 'W2': jax.random.normal(ks[13], (4 * D, D), jnp.float32) / np.sqrt(4 * D) * 0.1, 'b2': jnp.zeros((D,), jnp.float32)}
        return inp
    _L0_cond_all = _L0_cond_setup()
    _L0_cond_in = {k: v for k, v in _L0_cond_all.items() if k in ('Wm', 'bm', 'Lam_re', 'Lam_im', 'B_re', 'B_im', 'C_re', 'C_im', 'D_diag', 'log_step', 'Wc', 'bc', 'W1', 'b1', 'W2', 'b2')}
    del _L0_cond_all
    return {'x': x, 'cond_1024': cond_1024, 'L0_cond_Wm': _L0_cond_in['Wm'], 'L0_cond_bm': _L0_cond_in['bm'], 'L0_cond_Lam_re': _L0_cond_in['Lam_re'], 'L0_cond_Lam_im': _L0_cond_in['Lam_im'], 'L0_cond_B_re': _L0_cond_in['B_re'], 'L0_cond_B_im': _L0_cond_in['B_im'], 'L0_cond_C_re': _L0_cond_in['C_re'], 'L0_cond_C_im': _L0_cond_in['C_im'], 'L0_cond_D_diag': _L0_cond_in['D_diag'], 'L0_cond_log_step': _L0_cond_in['log_step'], 'L0_cond_Wc': _L0_cond_in['Wc'], 'L0_cond_bc': _L0_cond_in['bc'], 'L0_cond_W1': _L0_cond_in['W1'], 'L0_cond_b1': _L0_cond_in['b1'], 'L0_cond_W2': _L0_cond_in['W2'], 'L0_cond_b2': _L0_cond_in['b2']}

def reference(x, cond_1024, L0_cond_Wm, L0_cond_bm, L0_cond_Lam_re, L0_cond_Lam_im, L0_cond_B_re, L0_cond_B_im, L0_cond_C_re, L0_cond_C_im, L0_cond_D_diag, L0_cond_log_step, L0_cond_Wc, L0_cond_bc, L0_cond_W1, L0_cond_b1, L0_cond_W2, L0_cond_b2):
    import jax
    import jax.numpy as jnp

    def _L0_cond_ref(y, t, Wm, bm, Lam_re, Lam_im, B_re, B_im, C_re, C_im, D_diag, log_step, Wc, bc, W1, b1, W2, b2):
        import jax, jax.numpy as jnp
        import numpy as np
        B, L, D, P = (8, 512, 256, 64)

        def _ln(x):
            m = x.mean(-1, keepdims=True)
            v = x.var(-1, keepdims=True)
            return (x - m) * jax.lax.rsqrt(v + 1e-05)

        def _s5(u, Lam_re, Lam_im, B_re, B_im, C_re, C_im, D_diag, log_step):
            Lam = Lam_re + 1j * Lam_im
            dt = jnp.exp(log_step)
            Lam_bar = jnp.exp(Lam * dt)
            Bc = B_re + 1j * B_im
            B_bar = ((Lam_bar - 1.0) / Lam)[:, None] * Bc
            Bu = jnp.einsum('bld,pd->blp', u.astype(B_bar.dtype), B_bar)
            A = jnp.broadcast_to(Lam_bar, Bu.shape)

            def binop(e1, e2):
                a1, b1 = e1
                a2, b2 = e2
                return (a1 * a2, a2 * b1 + b2)
            _, xs = jax.lax.associative_scan(binop, (A, Bu), axis=1)
            Cc = C_re + 1j * C_im
            return 2.0 * jnp.einsum('blp,dp->bld', xs, Cc).real + D_diag * u
        mod = t @ Wm + bm
        shift_a, scale_a, gate_a, shift_ff, scale_ff, gate_ff = jnp.split(mod, 6, axis=-1)
        y_mod = _ln(y) * (1 + scale_a[:, None]) + shift_a[:, None]
        a_y = _s5(y_mod, Lam_re, Lam_im, B_re, B_im, C_re, C_im, D_diag, log_step)
        y = y + gate_a[:, None] * a_y
        cond = t @ Wc + bc
        scale_c, shift_c = jnp.split(cond, 2, axis=-1)
        y_norm = _ln(y) * (1 + scale_c[:, None]) + shift_c[:, None]
        y_mod = y_norm * (1 + scale_ff[:, None]) + shift_ff[:, None]
        h = jax.nn.gelu(y_mod @ W1 + b1)
        ff_y = h @ W2 + b2
        return y + gate_ff[:, None] * ff_y
    x = _L0_cond_ref(x, cond_1024, L0_cond_Wm, L0_cond_bm, L0_cond_Lam_re, L0_cond_Lam_im, L0_cond_B_re, L0_cond_B_im, L0_cond_C_re, L0_cond_C_im, L0_cond_D_diag, L0_cond_log_step, L0_cond_Wc, L0_cond_bc, L0_cond_W1, L0_cond_b1, L0_cond_W2, L0_cond_b2)
    return x

_drawn_inputs = setup_inputs


def setup_inputs(seed=0):
    import zlib

    import numpy as np

    out = dict(_drawn_inputs(seed))
    spreads = {'L0_cond_Lam_re': (-0.5, 0.6), 'L0_cond_b1': (0.0, 2.0), 'L0_cond_b2': (0.0, 0.294)}
    factors = {'L0_cond_bm': 2.789, 'L0_cond_Wc': 5.777, 'L0_cond_bc': 64.0}
    for name, (base, spread) in spreads.items():
        noise = np.random.default_rng([zlib.crc32(name.encode()), seed]).standard_normal(out[name].shape)
        drawn = base * np.exp(spread * noise) if base else spread * noise
        out[name] = jnp.asarray(drawn.astype(out[name].dtype))
    for name, factor in factors.items():
        out[name] = (out[name] * factor).astype(out[name].dtype)
    return out
```

```python
from contextlib import ExitStack

import concourse.bass as bass
from concourse import mybir

F32 = mybir.dt.float32
F32R = mybir.dt.float32r
I32 = mybir.dt.int32
ALU = mybir.AluOpType
ACT = mybir.ActivationFunctionType

LN_EPS = 1e-5
P = 128
TWO_PI_A = 6.28125
TWO_PI_B = 0.0019350051879882812
TWO_PI_C = 3.019916050561733e-07
INV_TWO_PI = 0.15915494309189535
TWO_PI_BELOW = 6.283185005187988
ROUND_TO_1 = 12582912.0
ROUND_TO_256TH = 49152.0
E_BASE = 2.7182817459106445
E_REST = 3.0367860004432146e-08


def cond_seq_kernel(nc, x, t, Wm, bm, Lam_re, Lam_im, B_re, B_im, C_re, C_im, D_diag, log_step,
                    Wc, bc, W1, b1, W2, b2, out):
    NB, L, D = x.shape
    S = Lam_re.shape[0]
    F = W1.shape[1]
    SEQ = 2
    GT = SEQ * L
    NG = NB // SEQ
    NT = GT // P
    ND = D // P
    NF = F // P
    NM = Wm.shape[1] // P
    NCC = Wc.shape[1] // P
    HS = 4
    LAG = 2
    assert 2 * S == P and GT == 512 and NG >= 6

    with ExitStack() as ctx:
        def sb(name, shape, dt=F32):
            return ctx.enter_context(nc.sbuf_tensor(name, shape, dt))

        def sem(name):
            return ctx.enter_context(nc.semaphore(name))

        ps_h = ctx.enter_context(nc.psum_tensor("ps_h", [P, 2, GT], F32))
        ps_ff = ctx.enter_context(nc.psum_tensor("ps_ff", [P, ND, GT], F32))
        ps_p = ctx.enter_context(nc.psum_tensor("ps_p", [P, 2, GT], F32))
        ps_q = ctx.enter_context(nc.psum_tensor("ps_q", [P, 2, GT], F32))

        ident = sb("ident", [P, P])
        step_i = sb("step_i", [P, L], I32)
        steps = sb("steps", [P, L])
        sign = sb("sign", [P, 1])
        c_rows = sb("c_rows", [P, ND, P])
        b_first = sb("b_first", [P, D])
        b_second = sb("b_second", [P, D])
        lam = sb("lam", [P, 3])
        w1 = sb("w1", [P, ND, F])
        w2 = sb("w2", [P, NF, D])
        w1h = sb("w1h", [P, ND, F], F32R)
        w1l = sb("w1l", [P, ND, F], F32R)
        w2h = sb("w2h", [P, NF, D], F32R)
        w2l = sb("w2l", [P, NF, D], F32R)
        wm = sb("wm", [P, ND, NM * P])
        wc = sb("wc", [P, ND, NCC * P])
        NV = NM + NCC + ND + ND + NF
        vec_rows = sb("vec_rows", [NV, P])
        vecs = sb("vecs", [P, NV])
        t_rows = sb("t_rows", [NB, D])
        t_cols = sb("t_cols", [P, ND, NB])
        mod = sb("mod", [P, NM + NCC, NB])
        scale_a = sb("scale_a", [P, ND, NB])
        scale_f1 = sb("scale_f1", [P, ND, NB])
        scale_v = sb("scale_v", [P, ND, NB])
        shift_v = sb("shift_v", [P, ND, NB])
        gate_b2 = sb("gate_b2", [P, ND, NB])
        sc = sb("sc", [P, 32])
        turn_f = sb("turn_f", [P, L])
        turn_w = sb("turn_w", [P, L])
        turn_c = sb("turn_c", [P, L])
        cos_t = sb("cos_t", [P, L])
        sin_t = sb("sin_t", [P, L])
        decay = sb("decay", [P, L])
        b_bar = sb("b_bar", [P, D])
        b_tmp = sb("b_tmp", [P, D])
        b_colT = sb("b_colT", [P, ND, P])
        c_colT = sb("c_colT", [P, ND, P])
        ln_eps = sb("ln_eps", [P, NT])
        carried = [sb(f"carried{n}", [P, 1]) for n in range(2)]
        minus_half = sb("minus_half", [P, NT])
        e_base = sb("e_base", [P, 1])

        xs = sb("xs", [P, NG, NT, D])
        stats = sb("stats", [P, NT, 6])
        mv_a = sb("mv_a", [P, NT, 2])
        mv_b = sb("mv_b", [P, NT, 2])
        var_a = sb("var_a", [P, NT])
        var_b = sb("var_b", [P, NT])
        rstd_a = sb("rstd_a", [P, NT])
        rstd_b = sb("rstd_b", [P, NT])
        stats_b = sb("stats_b", [P, NT, 6])
        xn = sb("xn", [P, NT, D])
        yn = sb("yn", [P, NT, D])
        u = sb("u", [P, ND, GT])
        bu_sw = sb("bu_sw", [P, GT])
        rot_c = sb("rot_c", [P, GT])
        rot_s = sb("rot_s", [P, GT])
        drive = sb("drive", [P, GT])
        z = sb("z", [P, GT])
        z_sw = sb("z_sw", [P, GT])
        back_c = sb("back_c", [P, GT])
        back_s = sb("back_s", [P, GT])
        state = sb("state", [P, GT])
        a_sum = sb("a_sum", [P, ND, GT])
        a_gated = sb("a_gated", [P, ND, GT])
        v = sb("v", [P, ND, GT])
        vh = sb("vh", [P, ND, GT], F32R)
        vl = sb("vl", [P, ND, GT], F32R)
        h = sb("h", [P, HS, GT])
        hh = sb("hh", [P, HS, GT], F32R)
        hl = sb("hl", [P, HS, GT], F32R)
        ff = sb("ff", [P, ND, GT])

        ld_small = sem("ld_small")
        ld_x0, ld_x1, ld_xrest = sem("ld_x0"), sem("ld_x1"), sem("ld_xrest")
        ld_wm, ld_w = sem("ld_wm"), sem("ld_w")
        stored = sem("stored")
        pool_consts = sem("pool_consts")
        vec_consts = sem("vec_consts")
        vec_step = sem("vec_step")
        pool_step = sem("pool_step")
        trig_made = sem("trig_made")
        setup_turned = sem("setup_turned")
        mod_summed = sem("mod_summed")
        w_high = sem("w_high")
        w_low = sem("w_low")
        stats_a = sem("stats_a")
        var_a_eps = sem("var_a_eps")
        rstd_a_made = sem("rstd_a_made")
        xn_made = sem("xn_made")
        xn_turned = sem("xn_turned")
        u_made = sem("u_made")
        bu_summed = sem("bu_summed")
        bu_swapped = sem("bu_swapped")
        rotated = sem("rotated")
        scanned = sem("scanned")
        z_swapped = sem("z_swapped")
        rotated_back = sem("rotated_back")
        state_made = sem("state_made")
        a_summed = sem("a_summed")
        a_sum_made = sem("a_sum_made")
        a_gated_made = sem("a_gated_made")
        a_turned = sem("a_turned")
        y1_made = sem("y1_made")
        stats_b_made = sem("stats_b_made")
        var_b_eps = sem("var_b_eps")
        rstd_b_made = sem("rstd_b_made")
        yn_made = sem("yn_made")
        yn_turned = sem("yn_turned")
        v_made = sem("v_made")
        v_high = sem("v_high")
        v_low = sem("v_low")
        f1_done = sem("f1_done")
        h_made = sem("h_made")
        h_high = sem("h_high")
        h_low = sem("h_low")
        f2_done = sem("f2_done")
        ff_made = sem("ff_made")
        ff_turned = sem("ff_turned")
        out_made = sem("out_made")

        x_rows = x.rearrange("(g h) (j p) d -> g p (h j) d", h=SEQ, p=P)
        out_rows = out.rearrange("(g h) (j p) d -> g p (h j) d", h=SEQ, p=P)
        col = lambda a: a.rearrange("(p o) -> p o", o=1)
        seq = lambda a, n: a[:, n * L:(n + 1) * L]
        HIGH, LOW = slice(0, S), slice(S, P)
        V_BM, V_BC, V_DD = 0, NM, NM + NCC
        V_B2, V_B1 = V_DD + ND, V_DD + 2 * ND
        SHIFT_A, SCALE_A, GATE_A, SHIFT_F, SCALE_F, GATE_F = range(0, NM, ND)
        SCALE_C, SHIFT_C = range(NM, NM + NCC, ND)

        def at_batch(tile, ct, g, n):
            return tile[:, ct, bass.ds(g * SEQ + n, 1)]

        def run(eng, tick, first, last):
            full_first, full_last = 3, NG - 1
            for k in range(first, full_first):
                tick(k)
            with eng.Fori(full_first, full_last + 1) as k:
                tick(k)
            for k in range(full_last + 1, last + 1):
                tick(k)

        def has(k, lag):
            return not isinstance(k, int) or 0 <= k - lag < NG

        block = ctx.enter_context(nc.Block())
        N_SMALL_LOADS = 1 + 5 + 6 + 2 + 4
        POOL_CONSTS, VEC_CONSTS = 3, 5
        VEC_RE_DT, VEC_TURNS, VEC_B_BAR, VEC_T_COLS, VEC_MOD = 3, 20, 37, 39, 49

        @block.sync
        def _(sp):
            with nc.allow_non_contiguous_dma(reason="small vectors, once"):
                sp.dma_start(t_rows[:, :], t).then_inc(ld_small, 16)
                for r, vec in ((V_BM, bm), (V_BC, bc), (V_DD, D_diag), (V_B2, b2), (V_B1, b1)):
                    rows = vec.rearrange("(r p) -> r p", p=P)
                    sp.dma_start(vec_rows[r:r + rows.shape[0], :], rows).then_inc(ld_small, 16)
                for n, vec in enumerate((Lam_re, Lam_im, log_step)):
                    for half in (HIGH, LOW):
                        sp.dma_start(lam[half, n:n + 1], col(vec)).then_inc(ld_small, 16)
            sp.dma_start(xs[:, 0], x_rows[0]).then_inc(ld_x0, 16)
            sp.dma_start(wm[:, :, :], Wm.rearrange("(k p) n -> p k n", p=P)).then_inc(ld_wm, 16)
            sp.dma_start(wc[:, :, :], Wc.rearrange("(k p) n -> p k n", p=P)).then_inc(ld_wm, 16)
            sp.dma_start(c_rows[:, :, 0:S], C_re.rearrange("(k p) s -> p k s", p=P)).then_inc(ld_small, 16)
            sp.dma_start(c_rows[:, :, S:P], C_im.rearrange("(k p) s -> p k s", p=P)).then_inc(ld_small, 16)
            for half, first, second in ((HIGH, B_re, B_im), (LOW, B_im, B_re)):
                sp.dma_start(b_first[half, :], first).then_inc(ld_small, 16)
                sp.dma_start(b_second[half, :], second).then_inc(ld_small, 16)
            sp.dma_start(xs[:, 1], x_rows[1]).then_inc(ld_x1, 16)
            sp.dma_start(w1[:, :, :], W1.rearrange("(k p) n -> p k n", p=P)).then_inc(ld_w, 16)
            sp.dma_start(w2[:, :, :], W2.rearrange("(k p) n -> p k n", p=P)).then_inc(ld_w, 16)
            for g in range(2, NG):
                sp.dma_start(xs[:, g], x_rows[g]).then_inc(ld_xrest, 16)
            with sp.Fori(0, NG) as g:
                sp.wait_ge(out_made, g * 2 + 2)
                sp.dma_start(out_rows[bass.ds(g, 1)].rearrange("g p n d -> (g p) n d"),
                             xs[:, bass.ds(g, 1)].rearrange("p g n d -> p (g n) d")).then_inc(stored, 16)
            sp.wait_ge(stored, 16 * NG)

        @block.gpsimd
        def _(pool):
            pool.iota(step_i[:, :], [[1, L]], base=0, channel_multiplier=0).then_inc(pool_consts, 1)
            pool.wait_ge(pool_consts, 1)
            pool.memset(ident[:, :], 0.0).then_inc(pool_consts, 1)
            pool.wait_ge(pool_consts, 2)
            pool.affine_select(ident[:, :], ident[:, :], pattern=[[-1, P]], compare_op=ALU.not_equal,
                               fill=1.0, base=0, channel_multiplier=1).then_inc(pool_consts, 1)
            pool.wait_ge(pool_consts, 3)
            pool.wait_ge(vec_consts, VEC_CONSTS)
            pool.wait_ge(ld_small, 16 * N_SMALL_LOADS)
            pool.tensor_tensor(sc[:, 0:1], e_base[:, :], lam[:, 2:3], ALU.pow).then_inc(pool_step, 1)
            pool.wait_ge(vec_step, VEC_RE_DT)
            pool.tensor_tensor(sc[:, 4:5], e_base[:, :], sc[:, 3:4], ALU.pow).then_inc(pool_step, 1)

            def rstd(k, stats_sem, mv, var, eps_sem, r, r_sem, g):
                pool.wait_ge(stats_sem, g * (2 * NT) + 2 * NT)
                pool.tensor_tensor(var[:, :], mv[:, :, 1], ln_eps[:, :], ALU.add).then_inc(eps_sem, 1)
                pool.wait_ge(eps_sem, g + 1)
                pool.tensor_tensor(r[:, :], var[:, :], minus_half[:, :], ALU.pow).then_inc(r_sem, 1)

            def low_weights():
                for n, (w, high, low) in enumerate(((w1, w1h, w1l), (w2, w2h, w2l))):
                    for m in range(4):
                        wf, hf, lf = (a[:, :, :].rearrange("p a b -> p (a b)")[:, m * 512:(m + 1) * 512]
                                      for a in (w, high, low))
                        pool.wait_ge(w_high, 4 * n + m + 1)
                        pool.tensor_tensor(lf, wf, hf.bitcast(F32), ALU.subtract).then_inc(w_low, 1)

            def tick(k):
                if has(k, 0):
                    rstd(k, stats_a, mv_a, var_a, var_a_eps, rstd_a, rstd_a_made, k)
                if isinstance(k, int) and k == 0:
                    low_weights()
                for f in range(NF):
                    if f == 3 and has(k, 1):
                        rstd(k, stats_b_made, mv_b, var_b, var_b_eps, rstd_b, rstd_b_made, k - 1)
                    if has(k, 2):
                        i = (k - 2) * NF + f
                        pool.wait_ge(h_high, i + 1)
                        if not (isinstance(k, int) and k == 2 and f < HS):
                            pool.wait_ge(f2_done, i + 1 - HS)
                        pool.tensor_tensor(hl[:, f % HS, :], h[:, f % HS, :], hh[:, f % HS, :].bitcast(F32),
                                           ALU.subtract).then_inc(h_low, 1)

            run(pool, tick, 0, NG + 1)

        @block.vector
        def _(dve):
            n_steps = [0]

            def step(ins, wait=True):
                n_steps[0] += 1
                ins.then_inc(vec_step, 1)
                if wait:
                    dve.wait_ge(vec_step, n_steps[0])
                return n_steps[0]

            dve.memset(sign[HIGH, :], 1.0).then_inc(vec_consts, 1)
            dve.memset(sign[LOW, :], -1.0).then_inc(vec_consts, 1)
            dve.memset(ln_eps[:, :], LN_EPS).then_inc(vec_consts, 1)
            dve.memset(minus_half[:, :], -0.5).then_inc(vec_consts, 1)
            dve.memset(e_base[:, :], E_BASE).then_inc(vec_consts, 1)
            dve.wait_ge(vec_consts, VEC_CONSTS)
            dve.wait_ge(pool_consts, POOL_CONSTS)
            c = lambda n: sc[:, n:n + 1]
            dve.wait_ge(ld_small, 16 * N_SMALL_LOADS)
            step(dve.tensor_scalar(c(1), lam[:, 2:3], E_REST, 1.0, ALU.mult, ALU.add))
            dve.wait_ge(pool_step, 1)
            step(dve.tensor_tensor(c(2), c(0), c(1), ALU.mult))
            assert step(dve.tensor_tensor(c(3), lam[:, 0:1], c(2), ALU.mult)) == VEC_RE_DT
            step(dve.tensor_tensor(c(5), lam[:, 1:2], c(2), ALU.mult))
            step(dve.tensor_scalar(c(6), c(5), INV_TWO_PI, ROUND_TO_256TH, ALU.mult, ALU.add))
            step(dve.tensor_scalar(c(7), c(6), -ROUND_TO_256TH, None, ALU.add))
            step(dve.scalar_tensor_tensor(out=c(8), in0=c(7), scalar=-TWO_PI_A, in1=c(5), op0=ALU.mult, op1=ALU.add))
            step(dve.scalar_tensor_tensor(out=c(9), in0=c(7), scalar=-TWO_PI_B, in1=c(8), op0=ALU.mult, op1=ALU.add))
            step(dve.scalar_tensor_tensor(out=c(10), in0=c(7), scalar=-TWO_PI_C, in1=c(9), op0=ALU.mult, op1=ALU.add))
            step(dve.tensor_scalar(c(11), c(10), INV_TWO_PI, None, ALU.mult))
            step(dve.tensor_copy(steps[:, :], step_i[:, :]))
            step(dve.tensor_scalar(turn_f[:, :], steps[:, :], c(7), None, ALU.mult))
            step(dve.tensor_scalar(turn_w[:, :], turn_f[:, :], ROUND_TO_1, -ROUND_TO_1, ALU.add, ALU.add))
            step(dve.tensor_tensor(turn_c[:, :], turn_f[:, :], turn_w[:, :], ALU.subtract))
            step(dve.scalar_tensor_tensor(out=turn_f[:, :], in0=steps[:, :], scalar=c(11), in1=turn_c[:, :],
                                          op0=ALU.mult, op1=ALU.add))
            step(dve.tensor_scalar(turn_w[:, :], turn_f[:, :], ROUND_TO_1, -ROUND_TO_1, ALU.add, ALU.add))
            step(dve.tensor_tensor(turn_c[:, :], turn_f[:, :], turn_w[:, :], ALU.subtract))
            step(dve.tensor_scalar(turn_f[:, :], turn_c[:, :], 0.25, None, ALU.add))
            step(dve.tensor_scalar(turn_w[:, :], turn_f[:, :], ROUND_TO_1, -ROUND_TO_1, ALU.add, ALU.add))
            step(dve.tensor_tensor(turn_f[:, :], turn_f[:, :], turn_w[:, :], ALU.subtract))
            assert n_steps[0] == VEC_TURNS
            step(dve.tensor_scalar(c(1), c(3), E_REST, 1.0, ALU.mult, ALU.add))
            dve.wait_ge(pool_step, 2)
            step(dve.tensor_tensor(c(12), c(4), c(1), ALU.mult))
            step(dve.tensor_scalar(decay[:, :], steps[:, :], 0.0, c(12), ALU.mult, ALU.add))
            dve.wait_ge(trig_made, 2)
            step(dve.tensor_scalar(sin_t[:, :], sin_t[:, :], sign[:, :], None, ALU.mult))
            step(dve.tensor_scalar(c(13), cos_t[:, 1:2], c(12), -1.0, ALU.mult, ALU.add))
            step(dve.tensor_scalar(c(14), sin_t[:, 1:2], c(12), sign[:, :], ALU.mult, ALU.mult))
            step(dve.tensor_tensor(c(15), lam[:, 0:1], lam[:, 0:1], ALU.mult))
            step(dve.scalar_tensor_tensor(out=c(16), in0=lam[:, 1:2], scalar=lam[:, 1:2], in1=c(15),
                                          op0=ALU.mult, op1=ALU.add))
            step(dve.reciprocal(c(17), c(16)))
            step(dve.tensor_tensor(c(18), c(14), lam[:, 1:2], ALU.mult))
            step(dve.scalar_tensor_tensor(out=c(19), in0=c(13), scalar=lam[:, 0:1], in1=c(18),
                                          op0=ALU.mult, op1=ALU.add))
            step(dve.tensor_tensor(c(20), c(19), c(17), ALU.mult))
            step(dve.tensor_tensor(c(21), c(13), lam[:, 1:2], ALU.mult))
            step(dve.scalar_tensor_tensor(out=c(22), in0=c(14), scalar=lam[:, 0:1], in1=c(21),
                                          op0=ALU.mult, op1=ALU.subtract))
            step(dve.tensor_scalar(c(23), c(22), c(17), sign[:, :], ALU.mult, ALU.mult))
            step(dve.tensor_scalar(b_tmp[:, :], b_second[:, :], c(23), None, ALU.mult))
            step(dve.scalar_tensor_tensor(out=b_bar[:, :], in0=b_first[:, :], scalar=c(20), in1=b_tmp[:, :],
                                          op0=ALU.mult, op1=ALU.subtract))
            assert n_steps[0] == VEC_B_BAR
            dve.wait_ge(setup_turned, 1)
            step(dve.tensor_copy(vecs[:, :], ps_p[:, 0, 0:NV]))
            step(dve.tensor_copy(t_cols[:, :, :], ps_p[:, 1, 0:ND * NB].rearrange("p (k b) -> p k b", b=NB)))
            assert n_steps[0] == VEC_T_COLS
            step(dve.tensor_scalar(c(24), sign[:, :], 2.0, None, ALU.mult))
            step(dve.tensor_scalar(c_colT[:, :, :], ps_p[:, 1, P:P + D].rearrange("p (k d) -> p k d", d=P),
                                   c(24), None, ALU.mult))
            dve.wait_ge(setup_turned, 2)
            step(dve.tensor_copy(b_colT[:, :, :], ps_q[:, 0, 0:D].rearrange("p (k d) -> p k d", d=P)))
            dve.wait_ge(mod_summed, 1)
            step(dve.tensor_tensor(mod[:, :, :],
                                   ps_ff[:, 0, 0:(NM + NCC) * NB].rearrange("p (c b) -> p c b", b=NB),
                                   vecs[:, V_BM:V_DD].unsqueeze(2).to_broadcast([P, NM + NCC, NB]), ALU.add))
            part = lambda ct: mod[:, ct:ct + ND, :]
            step(dve.tensor_scalar(scale_a[:, :, :], part(SCALE_A), 1.0, None, ALU.add))
            step(dve.tensor_scalar(scale_f1[:, :, :], part(SCALE_F), 1.0, None, ALU.add))
            step(dve.scalar_tensor_tensor(out=scale_v[:, :, :], in0=part(SCALE_C), scalar=1.0,
                                          in1=scale_f1[:, :, :], op0=ALU.add, op1=ALU.mult))
            step(dve.tensor_tensor(shift_v[:, :, :], part(SHIFT_C), scale_f1[:, :, :], ALU.mult))
            step(dve.tensor_tensor(shift_v[:, :, :], shift_v[:, :, :], part(SHIFT_F), ALU.add))
            step(dve.tensor_tensor(gate_b2[:, :, :], part(GATE_F),
                                   vecs[:, V_B2:V_B2 + ND].unsqueeze(2).to_broadcast([P, ND, NB]), ALU.mult))
            assert n_steps[0] == VEC_MOD

            def carry(scratch):
                dve.tensor_copy(scratch[:, :], sign[:, :])

            def norm_stats(xg, st, mv, done, g):
                for n in range(NT):
                    dve.bn_stats(st[:, n, :], xg[:, n, :]).then_inc(done, 1)
                dve.wait_ge(done, g * (2 * NT) + NT)
                carry(carried[1])
                for n in range(NT):
                    dve.bn_aggr(mv[:, n, :], st[:, n, :]).then_inc(done, 1)

            def normalise(dst, xg, mv, r, done):
                for n in range(NT):
                    dve.tensor_scalar(dst[:, n, :], xg[:, n, :], mv[:, n, 0:1], r[:, n:n + 1],
                                      ALU.subtract, ALU.mult).then_inc(done, 1)

            def rows(g):
                return xs[:, bass.ds(g, 1)].rearrange("p g n d -> p (g n) d")

            def tick(k):
                a, b, c = k, k - 1, k - 2
                if has(k, 1):
                    dve.wait_ge(a_summed, b + 1)
                    for d in range(ND):
                        dve.scalar_tensor_tensor(out=a_sum[:, d, :], in0=u[:, d, :],
                                                 scalar=vecs[:, V_DD + d:V_DD + d + 1], in1=ps_p[:, d, :],
                                                 op0=ALU.mult, op1=ALU.add).then_inc(a_sum_made, 1)
                if has(k, 0):
                    if isinstance(k, int) and k < 3:
                        dve.wait_ge((ld_x0, ld_x1, ld_xrest)[k], (16, 16, 16 * (NG - 2))[k])
                    norm_stats(rows(a), stats, mv_a, stats_a, a)
                if has(k, 3):
                    dve.wait_ge(ff_turned, c)
                    for n in range(2):
                        xg = rows(c - 1)[:, 2 * n:2 * n + 2, :]
                        dve.tensor_tensor(xg, xg, ps_q[:, n, :].rearrange("p (j d) -> p j d", d=D),
                                          ALU.add).then_inc(out_made, 1)
                if has(k, 0):
                    dve.wait_ge(rstd_a_made, a + 1)
                    normalise(xn, rows(a), mv_a, rstd_a, xn_made)
                if has(k, 1):
                    dve.wait_ge(a_turned, b + 1)
                    for n in range(2):
                        xg = rows(b)[:, 2 * n:2 * n + 2, :]
                        dve.tensor_tensor(xg, xg, ps_q[:, n, :].rearrange("p (j d) -> p j d", d=D),
                                          ALU.add).then_inc(y1_made, 1)
                    dve.wait_ge(y1_made, b * 2 + 2)
                    carry(carried[0])
                    norm_stats(rows(b), stats_b, mv_b, stats_b_made, b)
                if has(k, 0):
                    dve.wait_ge(bu_swapped, a * 2 + 2)
                    wide = lambda tile: tile[:, :].unsqueeze(1).to_broadcast([P, SEQ, L])
                    three = lambda ap: ap.rearrange("p (s l) -> p s l", l=L)
                    dve.tensor_tensor(three(rot_c[:, :]), three(ps_p[:, 0, :]), wide(cos_t), ALU.mult)\
                       .then_inc(rotated, 1)
                    dve.tensor_tensor(three(rot_s[:, :]), three(bu_sw[:, :]), wide(sin_t), ALU.mult)\
                       .then_inc(rotated, 1)
                    dve.wait_ge(rotated, a * 3 + 2)
                    dve.tensor_tensor(drive[:, :], rot_c[:, :], rot_s[:, :], ALU.add).then_inc(rotated, 1)
                    dve.wait_ge(rotated, a * 3 + 3)
                    for n in range(SEQ):
                        dve.tensor_tensor_scan(seq(z, n), decay[:, :], seq(drive, n), 0.0,
                                               ALU.mult, ALU.add).then_inc(scanned, 1)
                if has(k, 1):
                    dve.wait_ge(rstd_b_made, b + 1)
                    normalise(yn, rows(b), mv_b, rstd_b, yn_made)
                if has(k, 0):
                    dve.wait_ge(scanned, a * SEQ + SEQ)
                    dve.tensor_tensor(three(back_c[:, :]), three(z[:, :]), wide(cos_t), ALU.mult)\
                       .then_inc(rotated_back, 1)
                    dve.wait_ge(z_swapped, a * 2 + 2)
                    dve.tensor_tensor(three(back_s[:, :]), three(z_sw[:, :]), wide(sin_t), ALU.mult)\
                       .then_inc(rotated_back, 1)
                    dve.wait_ge(rotated_back, a * 2 + 2)
                    dve.tensor_tensor(state[:, :], back_c[:, :], back_s[:, :], ALU.subtract)\
                       .then_inc(state_made, 1)
                if has(k, 1):
                    if has(k, 2):
                        dve.wait_ge(f1_done, c * NF + NF)
                    for d in range(ND):
                        dve.wait_ge(v_made, b * (ND * SEQ) + SEQ * (d + 1))
                        dve.tensor_copy(vh[:, d, :], v[:, d, :]).then_inc(v_high, 1)
                    for d in range(ND):
                        dve.wait_ge(v_high, b * ND + d + 1)
                        dve.tensor_tensor(vl[:, d, :], v[:, d, :], vh[:, d, :].bitcast(F32), ALU.subtract)\
                           .then_inc(v_low, 1)

            run(dve, tick, 0, NG + 2)

        @block.scalar
        def _(act):
            act.wait_ge(vec_step, VEC_TURNS)
            act.activation(sin_t[:, :], turn_c[:, :], ACT.Sin, scale=TWO_PI_BELOW).then_inc(trig_made, 1)
            act.activation(cos_t[:, :], turn_f[:, :], ACT.Sin, scale=TWO_PI_BELOW).then_inc(trig_made, 1)
            act.preload_act_table(ACT.Gelu_apprx_tanh)
            act.wait_ge(ld_w, 32)
            for w, high in ((w1, w1h), (w2, w2h)):
                for m in range(4):
                    wf, hf = (a[:, :, :].rearrange("p a b -> p (a b)")[:, m * 512:(m + 1) * 512] for a in (w, high))
                    act.activation(hf, wf, ACT.Copy).then_inc(w_high, 1)
            act.wait_ge(vec_step, VEC_MOD)

            def gelu(k, f):
                if not has(k, 2):
                    return
                i = (k - 2) * NF + f
                act.wait_ge(f1_done, i + 1)
                if not (isinstance(k, int) and k == 2 and f < HS):
                    act.wait_ge(h_low, i + 1 - HS)
                    act.wait_ge(f2_done, i + 1 - HS)
                bias = vecs[:, V_B1 + f:V_B1 + f + 1]
                act.activation(h[:, f % HS, :], ps_h[:, f % 2, :], ACT.Gelu_apprx_tanh, bias=bias).then_inc(h_made, 1)
                act.activation(hh[:, f % HS, :], ps_h[:, f % 2, :], ACT.Gelu_apprx_tanh, bias=bias).then_inc(h_high, 1)

            def swap_halves(dst, src, done):
                act.activation(dst[HIGH, :], src[LOW, :], ACT.Copy).then_inc(done, 1)
                act.activation(dst[LOW, :], src[HIGH, :], ACT.Copy).then_inc(done, 1)

            def tick(k):
                a, b, c = k, k - 1, k - 2
                if has(k, 3):
                    act.wait_ge(f2_done, c * NF)
                    for d in range(ND):
                        for n in range(SEQ):
                            act.activation(ff[:, d, n * L:(n + 1) * L], ps_ff[:, d, n * L:(n + 1) * L], ACT.Identity,
                                           scale=at_batch(mod, GATE_F + d, c - 1, n),
                                           bias=at_batch(gate_b2, d, c - 1, n)).then_inc(ff_made, 1)
                if has(k, 1):
                    act.wait_ge(a_sum_made, b * ND + ND)
                    for d in range(ND):
                        for n in range(SEQ):
                            act.activation(a_gated[:, d, n * L:(n + 1) * L], a_sum[:, d, n * L:(n + 1) * L], ACT.Copy,
                                           scale=at_batch(mod, GATE_A + d, b, n)).then_inc(a_gated_made, 1)
                gelu(k, 0)
                gelu(k, 1)
                if has(k, 0):
                    act.wait_ge(xn_turned, a + 1)
                    for d in range(ND):
                        for n in range(SEQ):
                            act.activation(u[:, d, n * L:(n + 1) * L], ps_p[:, d, n * L:(n + 1) * L], ACT.Identity,
                                           scale=at_batch(scale_a, d, a, n),
                                           bias=at_batch(mod, SHIFT_A + d, a, n)).then_inc(u_made, 1)
                gelu(k, 2)
                gelu(k, 3)
                if has(k, 0):
                    act.wait_ge(bu_summed, a + 1)
                    swap_halves(bu_sw, ps_p[:, 0, :], bu_swapped)
                gelu(k, 4)
                gelu(k, 5)
                if has(k, 0):
                    act.wait_ge(scanned, a * SEQ + SEQ)
                    swap_halves(z_sw, z, z_swapped)
                gelu(k, 6)
                if has(k, 1):
                    act.wait_ge(yn_turned, b + 1)
                    for d in range(ND):
                        for n in range(SEQ):
                            act.activation(v[:, d, n * L:(n + 1) * L], ps_q[:, d, n * L:(n + 1) * L], ACT.Identity,
                                           scale=at_batch(scale_v, d, b, n),
                                           bias=at_batch(shift_v, d, b, n)).then_inc(v_made, 1)
                gelu(k, 7)

            run(act, tick, 0, NG + 2)

        @block.tensor
        def _(pe):
            pe.wait_ge(pool_consts, POOL_CONSTS)
            pe.wait_ge(ld_small, 16 * N_SMALL_LOADS)
            pe.transpose(ps_p[:, 0, 0:NV], vec_rows[:, :], ident[0:NV, 0:NV])
            for d in range(ND):
                pe.transpose(ps_p[:, 1, d * NB:(d + 1) * NB], t_rows[:, d * P:(d + 1) * P], ident[0:NB, 0:NB])
            for d in range(ND):
                last = pe.transpose(ps_p[:, 1, P + d * P:P + (d + 1) * P], c_rows[:, d, :], ident[:, :])
            last.then_inc(setup_turned, 1)
            pe.wait_ge(vec_step, VEC_B_BAR)
            for d in range(ND):
                last = pe.transpose(ps_q[:, 0, d * P:(d + 1) * P], b_bar[:, d * P:(d + 1) * P], ident[:, :])
            last.then_inc(setup_turned, 1)
            pe.wait_ge(ld_wm, 32)
            pe.wait_ge(vec_step, VEC_T_COLS)
            for ct in range(NM + NCC):
                w, m = (wm, ct) if ct < NM else (wc, ct - NM)
                for kt in range(ND):
                    last = pe.matmul(ps_ff[:, 0, ct * NB:(ct + 1) * NB], w[:, kt, m * P:(m + 1) * P],
                                     t_cols[:, kt, :], start=(kt == 0), stop=(kt == ND - 1))
            last.then_inc(mod_summed, 1)
            pe.wait_ge(vec_step, VEC_MOD)

            def split_product(dst, wh, wl, ah, al, start, stop):
                pe.matmul(dst, wl, ah, start=start, stop=False)
                pe.matmul(dst, wh, al, start=False, stop=False)
                return pe.matmul(dst, wh, ah, start=False, stop=stop)

            def f1(k, f):
                if not has(k, 2):
                    return
                c = k - 2
                i = c * NF + f
                if f == 0:
                    pe.wait_ge(v_low, c * ND + ND)
                    if isinstance(k, int) and k == 2:
                        pe.wait_ge(w_low, 8)
                if not (isinstance(k, int) and k == 2 and f < 2):
                    pe.wait_ge(h_high, i - 1)
                for kt in range(ND):
                    fs = slice(f * P, (f + 1) * P)
                    last = split_product(ps_h[:, f % 2, :], w1h[:, kt, fs], w1l[:, kt, fs], vh[:, kt, :], vl[:, kt, :],
                                         kt == 0, kt == ND - 1)
                last.then_inc(f1_done, 1)

            def f2(k, f):
                if not has(k, 2):
                    return
                i = (k - 2) * NF + f
                pe.wait_ge(h_low, i + 1)
                for d in range(ND):
                    ds = slice(d * P, (d + 1) * P)
                    last = split_product(ps_ff[:, d, :], w2h[:, f, ds], w2l[:, f, ds], hh[:, f % HS, :], hl[:, f % HS, :],
                                         f == 0, f == NF - 1)
                last.then_inc(f2_done, 1)

            def turn_to_columns(dst, src, done):
                for d in range(ND):
                    for n in range(NT):
                        last = pe.transpose(dst[:, d, n * P:(n + 1) * P], src[:, n, d * P:(d + 1) * P], ident[:, :])
                last.then_inc(done, 1)

            def turn_to_rows(dst, src, done):
                for n in range(NT):
                    for d in range(ND):
                        last = pe.transpose(dst[:, n // 2, (n % 2) * D + d * P:(n % 2) * D + (d + 1) * P],
                                            src[:, d, n * P:(n + 1) * P], ident[:, :])
                last.then_inc(done, 1)

            def tick(k):
                a, b, c = k, k - 1, k - 2
                if has(k, 1):
                    pe.wait_ge(state_made, b + 1)
                    for d in range(ND):
                        last = pe.matmul(ps_p[:, d, :], c_colT[:, d, :], state[:, :], start=True, stop=True)
                    last.then_inc(a_summed, 1)
                f1(k, 0)
                f1(k, 1)
                if has(k, 3):
                    pe.wait_ge(ff_made, c * (ND * SEQ))
                    if has(k, 2):
                        pe.wait_ge(v_made, b * (ND * SEQ))
                    else:
                        pe.wait_ge(out_made, (c - 1) * 2)
                    turn_to_rows(ps_q, ff, ff_turned)
                if has(k, 0):
                    pe.wait_ge(xn_made, a * NT + NT)
                    if has(k, 1):
                        pe.wait_ge(a_sum_made, b * ND + ND)
                    turn_to_columns(ps_p, xn, xn_turned)
                f1(k, 2)
                f2(k, 0)
                if has(k, 1):
                    pe.wait_ge(a_gated_made, b * (ND * SEQ) + ND * SEQ)
                    if has(k, 3):
                        pe.wait_ge(out_made, c * 2)
                    turn_to_rows(ps_q, a_gated, a_turned)
                f1(k, 3)
                f2(k, 1)
                if has(k, 0):
                    pe.wait_ge(u_made, a * (ND * SEQ) + ND * SEQ)
                    for kt in range(ND):
                        last = pe.matmul(ps_p[:, 0, :], b_colT[:, kt, :], u[:, kt, :], start=(kt == 0),
                                         stop=(kt == ND - 1))
                    last.then_inc(bu_summed, 1)
                f1(k, 4)
                f2(k, 2)
                f1(k, 5)
                f2(k, 3)
                f1(k, 6)
                f2(k, 4)
                if has(k, 1):
                    pe.wait_ge(yn_made, b * NT + NT)
                    turn_to_columns(ps_q, yn, yn_turned)
                f1(k, 7)
                f2(k, 5)
                f2(k, 6)
                f2(k, 7)

            run(pe, tick, 0, NG + 2)


_INS = ['x', 'cond_1024'] + ['L0_cond_' + n for n in (
    'Wm', 'bm', 'Lam_re', 'Lam_im', 'B_re', 'B_im', 'C_re', 'C_im', 'D_diag', 'log_step', 'Wc', 'bc', 'W1', 'b1', 'W2', 'b2')]


def kernel(**inputs):
    import numpy as np
    import concourse.bacc as bacc
    from concourse.bass_utils import run_bass_kernel_spmd

    nc = bacc.Bacc("TRN2", target_bir_lowering=False, num_devices=1)
    arrays, args = {}, []
    for name in _INS:
        a = np.ascontiguousarray(inputs[name])
        arrays["in_" + name] = a
        args.append(nc.dram_tensor("in_" + name, a.shape, mybir.dt.from_np(a.dtype), kind="ExternalInput").ap())
    shape = inputs["x"].shape
    args.append(nc.dram_tensor("out_y", shape, F32, kind="ExternalOutput").ap())
    cond_seq_kernel(nc, *args)
    r = run_bass_kernel_spmd(nc, [arrays], core_ids=[0])
    return r.results[0]["out_y"]
```

```python
from contextlib import ExitStack

import concourse.bass as bass
from concourse import mybir

F32 = mybir.dt.float32
F32R = mybir.dt.float32r
ALU = mybir.AluOpType
ACT = mybir.ActivationFunctionType

LN_EPS = 1e-5
P = 128
TWO_PI_A = 6.28125
TWO_PI_B = 0.0019350051879882812
TWO_PI_C = 3.019916050561733e-07
INV_TWO_PI = 0.15915494309189535
TWO_PI_BELOW = 6.283185005187988
ROUND_TO_1 = 12582912.0
ROUND_TO_256TH = 49152.0
E_BASE = 2.7182817459106445
E_REST = 3.0367860004432146e-08


def cond_seq_kernel(nc, x, t, Wm, bm, Lam_re, Lam_im, B_re, B_im, C_re, C_im, D_diag, log_step,
                    Wc, bc, W1, b1, W2, b2, out):
    NB, L, D = x.shape
    S = Lam_re.shape[0]
    F = W1.shape[1]
    SEQ = 2
    GT = SEQ * L
    NG = NB // SEQ
    NT = GT // P
    ND = D // P
    NF = F // P
    NM = Wm.shape[1] // P
    NCC = Wc.shape[1] // P
    HS = 4
    LAG = 2
    assert 2 * S == P and GT == 512 and NG >= 6

    with ExitStack() as ctx:
        def sb(name, shape, dt=F32):
            return ctx.enter_context(nc.sbuf_tensor(name, shape, dt))

        def sem(name):
            return ctx.enter_context(nc.semaphore(name))

        ps_h = ctx.enter_context(nc.psum_tensor("ps_h", [P, 2, GT], F32))
        ps_ff = ctx.enter_context(nc.psum_tensor("ps_ff", [P, ND, GT], F32))
        ps_p = ctx.enter_context(nc.psum_tensor("ps_p", [P, 2, GT], F32))
        ps_q = ctx.enter_context(nc.psum_tensor("ps_q", [P, 2, GT], F32))

        ident = sb("ident", [P, P])
        steps = sb("steps", [P, L])
        sign = sb("sign", [P, 1])
        ln_eps = sb("ln_eps", [P, NT])
        minus_half = sb("minus_half", [P, NT])
        e_base = sb("e_base", [P, 1])
        c_rows = sb("c_rows", [P, ND, P])
        b_first = sb("b_first", [P, D])
        b_second = sb("b_second", [P, D])
        w1 = sb("w1", [P, ND, F])
        w1h, w1l = sb("w1h", [P, ND, F], F32R), sb("w1l", [P, ND, F], F32R)
        w2h, w2l = sb("w2h", [P, NF, D], F32R), sb("w2l", [P, NF, D], F32R)
        wm = sb("wm", [P, ND, NM * P])
        wc = sb("wc", [P, ND, NCC * P])
        NV1, NV2 = 3 + NM, NCC + ND + ND + NF
        vec_rows1, vec_rows2 = sb("vec_rows1", [NV1, P]), sb("vec_rows2", [NV2, P])
        vecs = sb("vecs", [P, NV1 + NV2])
        t_rows = sb("t_rows", [NB, D])
        t_cols = sb("t_cols", [P, ND, NB])
        mod = sb("mod", [P, NM + NCC, NB])
        scale_a = sb("scale_a", [P, ND, NB])
        scale_f1 = sb("scale_f1", [P, ND, NB])
        scale_v = sb("scale_v", [P, ND, NB])
        shift_v1 = sb("shift_v1", [P, ND, NB])
        shift_v = sb("shift_v", [P, ND, NB])
        gate_b2 = sb("gate_b2", [P, ND, NB])
        sc = sb("sc", [P, 32])
        turn_f = sb("turn_f", [P, L])
        turn_c = sb("turn_c", [P, L])
        turns = sb("turns", [P, 2, L])
        turns_w = sb("turns_w", [P, 2, L])
        turns_r = sb("turns_r", [P, 2, L])
        cos_t = sb("cos_t", [P, L])
        sin_raw = sb("sin_raw", [P, L])
        sin_t = sb("sin_t", [P, L])
        decay = sb("decay", [P, L])
        b_bar = sb("b_bar", [P, D])
        b_tmp = sb("b_tmp", [P, D])
        bT = sb("bT", [P, ND, P])
        bTh, bTl = sb("bTh", [P, ND, P], F32R), sb("bTl", [P, ND, P], F32R)
        cT = sb("cT", [P, ND, P])
        cTh, cTl = sb("cTh", [P, ND, P], F32R), sb("cTl", [P, ND, P], F32R)
        carried = [sb(f"carried{n}", [P, 1]) for n in range(2)]

        xs = sb("xs", [P, NG, NT, D])
        stats_a, stats_b = sb("stats_a", [P, NT, 6]), sb("stats_b", [P, NT, 6])
        mv_a, mv_b = sb("mv_a", [P, NT, 2]), sb("mv_b", [P, NT, 2])
        var_a, var_b = sb("var_a", [P, NT]), sb("var_b", [P, NT])
        rstd_a, rstd_b = sb("rstd_a", [P, NT]), sb("rstd_b", [P, NT])
        xn = sb("xn", [P, NT, D])
        yn = sb("yn", [P, NT, D])
        u = sb("u", [P, ND, GT])
        uh, ul = sb("uh", [P, ND, GT], F32R), sb("ul", [P, ND, GT], F32R)
        bu_sw = sb("bu_sw", [P, GT])
        rot_c = sb("rot_c", [P, GT])
        rot_s = sb("rot_s", [P, GT])
        drive = sb("drive", [P, GT])
        z = sb("z", [P, GT])
        z_sw = sb("z_sw", [P, GT])
        back_c = sb("back_c", [P, GT])
        back_s = sb("back_s", [P, GT])
        state = sb("state", [P, GT])
        state_h, state_l = sb("state_h", [P, GT], F32R), sb("state_l", [P, GT], F32R)
        a_sum = sb("a_sum", [P, ND, GT])
        a_gated = sb("a_gated", [P, ND, GT])
        v = sb("v", [P, ND, GT])
        vh, vl = sb("vh", [P, ND, GT], F32R), sb("vl", [P, ND, GT], F32R)
        h = sb("h", [P, HS, GT])
        w2 = h[:, :, :].rearrange("p s (k n) -> p (s k) n", n=D)
        hh, hl = sb("hh", [P, HS, GT], F32R), sb("hl", [P, HS, GT], F32R)
        ff = sb("ff", [P, ND, GT])

        x_loaded = [sem("x0_loaded"), sem("x1_loaded"), sem("x_rest_loaded")]
        vecs_loaded = sem("vecs_loaded")
        vecs2_loaded = sem("vecs2_loaded")
        bc_loaded = sem("bc_loaded")
        wa_loaded = sem("wa_loaded")
        wm_loaded = sem("wm_loaded")
        w_loaded = [sem("w1_loaded"), sem("w2_loaded")]
        stored = sem("stored")
        pool_consts = sem("pool_consts")
        vec_consts = sem("vec_consts")
        own_step = sem("own_step")
        vecs_turned = sem("vecs_turned")
        vecs_made = sem("vecs_made")
        dt_raised = sem("dt_raised")
        re_dt_made = sem("re_dt_made")
        mag_raised = sem("mag_raised")
        turns_made = sem("turns_made")
        trig_made = sem("trig_made")
        mod_a_summed = sem("mod_a_summed")
        mod_a_made = sem("mod_a_made")
        b_bar_made = sem("b_bar_made")
        b_turned = sem("b_turned")
        b_parts = sem("b_parts")
        c_turned = sem("c_turned")
        c_parts = sem("c_parts")
        mod_summed = sem("mod_summed")
        mod_made = sem("mod_made")
        vecs2_made = sem("vecs2_made")
        w_high = sem("w_high")
        w_low = sem("w_low")
        stats_a_made = sem("stats_a_made")
        var_a_eps = sem("var_a_eps")
        rstd_a_made = sem("rstd_a_made")
        xn_made = sem("xn_made")
        xn_turned = sem("xn_turned")
        u_made = sem("u_made")
        u_high = sem("u_high")
        u_low = sem("u_low")
        bu_summed = sem("bu_summed")
        bu_swapped = sem("bu_swapped")
        rotated = sem("rotated")
        scanned = sem("scanned")
        z_swapped = sem("z_swapped")
        rotated_back = sem("rotated_back")
        state_made = sem("state_made")
        state_high = sem("state_high")
        state_low = sem("state_low")
        a_summed = sem("a_summed")
        a_sum_made = sem("a_sum_made")
        a_gated_made = sem("a_gated_made")
        a_turned = sem("a_turned")
        y1_made = sem("y1_made")
        stats_b_made = sem("stats_b_made")
        var_b_eps = sem("var_b_eps")
        rstd_b_made = sem("rstd_b_made")
        yn_made = sem("yn_made")
        yn_turned = sem("yn_turned")
        v_made_act = sem("v_made_act")
        v_made_dve = sem("v_made_dve")
        v_high = sem("v_high")
        v_low = sem("v_low")
        f1_done = sem("f1_done")
        h_made = sem("h_made")
        h_high = sem("h_high")
        h_low = sem("h_low")
        f2_done = sem("f2_done")
        ff_made = sem("ff_made")
        ff_turned = sem("ff_turned")
        out_made = sem("out_made")

        x_rows = x.rearrange("(g h) (j p) d -> g p (h j) d", h=SEQ, p=P)
        out_rows = out.rearrange("(g h) (j p) d -> g p (h j) d", h=SEQ, p=P)
        HIGH, LOW = slice(0, S), slice(S, P)
        V_LAM_RE, V_LAM_IM, V_LOG_STEP, V_BM = range(4)
        V_BC = NV1
        V_DD, V_B2, V_B1 = range(V_BC + NCC, V_BC + NCC + 3 * ND, ND)
        vec = lambda r: vecs[:, r:r + 1]
        SHIFT_A, SCALE_A, GATE_A, SHIFT_F, SCALE_F, GATE_F = range(0, NM, ND)
        SCALE_C, SHIFT_C = range(NM, NM + NCC, ND)
        NA = 2 * ND
        N_VEC_LOADS, N_BC_LOADS = 5, 2 + 4
        POOL_CONSTS, VEC_CONSTS = 3, 5

        def seq(tile, n):
            return tile[..., n * L:(n + 1) * L]

        def at_batch(table, ct, g, n):
            return table[:, ct, bass.ds(g * SEQ + n, 1)]

        def rows(g):
            return xs[:, bass.ds(g, 1)].rearrange("p g n d -> p (g n) d")

        def run(eng, tick, last):
            full_first, full_last = 3, NG - 2
            for k in range(full_first):
                tick(k)
            with eng.Fori(full_first, full_last + 1) as k:
                tick(k)
            for k in range(full_last + 1, last + 1):
                tick(k)

        def has(k, lag):
            return not isinstance(k, int) or 0 <= k - lag < NG

        def is_tick(k, n):
            return isinstance(k, int) and k == n

        block = ctx.enter_context(nc.Block())

        @block.sync
        def _(sp):
            def load_vec(rows_tile, r, a, done):
                a = a.rearrange("(r p) -> r p", p=P)
                sp.dma_start(rows_tile[r:r + a.shape[0], :], a).then_inc(done, 16)

            for r, a in ((V_LAM_RE, Lam_re), (V_LAM_IM, Lam_im), (V_LOG_STEP, log_step)):
                sp.dma_start(vec_rows1[r:r + 1, :].rearrange("o (h s) -> o h s", s=S),
                             a.rearrange("(o h s) -> o h s", o=1, h=1).to_broadcast([1, 2, S])).then_inc(vecs_loaded, 16)
            sp.dma_start(t_rows[:, :], t).then_inc(vecs_loaded, 16)
            load_vec(vec_rows1, V_BM, bm, vecs_loaded)
            sp.dma_start(xs[:, 0], x_rows[0]).then_inc(x_loaded[0], 16)
            wm_cols = Wm.rearrange("(k p) n -> p k n", p=P)
            sp.dma_start(wm[:, :, 0:NA * P], wm_cols[:, :, 0:NA * P]).then_inc(wa_loaded, 16)
            for half, first, second in ((HIGH, B_re, B_im), (LOW, B_im, B_re)):
                sp.dma_start(b_first[half, :], first).then_inc(bc_loaded, 16)
                sp.dma_start(b_second[half, :], second).then_inc(bc_loaded, 16)
            sp.dma_start(c_rows[:, :, 0:S], C_re.rearrange("(k p) s -> p k s", p=P)).then_inc(bc_loaded, 16)
            sp.dma_start(c_rows[:, :, S:P], C_im.rearrange("(k p) s -> p k s", p=P)).then_inc(bc_loaded, 16)
            sp.dma_start(wm[:, :, NA * P:], wm_cols[:, :, NA * P:]).then_inc(wm_loaded, 16)
            sp.dma_start(wc[:, :, :], Wc.rearrange("(k p) n -> p k n", p=P)).then_inc(wm_loaded, 16)
            for v_col, a in ((V_BC, bc), (V_DD, D_diag), (V_B2, b2), (V_B1, b1)):
                load_vec(vec_rows2, v_col - NV1, a, vecs2_loaded)
            sp.dma_start(xs[:, 1], x_rows[1]).then_inc(x_loaded[1], 16)
            sp.dma_start(w1[:, :, :], W1.rearrange("(k p) n -> p k n", p=P)).then_inc(w_loaded[0], 16)
            sp.dma_start(w2, W2.rearrange("(k p) n -> p k n", p=P)).then_inc(w_loaded[1], 16)
            for g in range(2, NG):
                sp.dma_start(xs[:, g], x_rows[g]).then_inc(x_loaded[2], 16)
            with sp.Fori(0, NG) as g:
                for n in range(2):
                    half = slice(2 * n, 2 * n + 2)
                    sp.wait_ge(out_made, g * 2 + n + 1)
                    sp.dma_start(out_rows[bass.ds(g, 1), :, half, :].rearrange("g p n d -> (g p) n d"),
                                 rows(g)[:, half, :]).then_inc(stored, 16)
            sp.wait_ge(stored, 16 * 2 * NG)

        @block.gpsimd
        def _(pool):
            pool.iota(steps[:, :], [[1, L]], base=0, channel_multiplier=0,
                      allow_small_or_imprecise_dtypes=True).then_inc(pool_consts, 1)
            pool.wait_ge(pool_consts, 1)
            pool.memset(ident[:, :], 0.0).then_inc(pool_consts, 1)
            pool.wait_ge(pool_consts, 2)
            pool.affine_select(ident[:, :], ident[:, :], pattern=[[-1, P]], compare_op=ALU.not_equal,
                               fill=1.0, base=0, channel_multiplier=1).then_inc(pool_consts, 1)

            def rstd(g, stats_sem, mv, var, eps_sem, r, r_sem):
                pool.wait_ge(stats_sem, g * (2 * NT) + 2 * NT)
                pool.tensor_tensor(var[:, :], mv[:, :, 1], ln_eps[:, :], ALU.add).then_inc(eps_sem, 1)
                pool.wait_ge(eps_sem, g + 1)
                pool.tensor_tensor(r[:, :], var[:, :], minus_half[:, :], ALU.pow).then_inc(r_sem, 1)

            def rstd_of_x(g):
                rstd(g, stats_a_made, mv_a, var_a, var_a_eps, rstd_a, rstd_a_made)

            def rstd_of_y1(g):
                rstd(g, stats_b_made, mv_b, var_b, var_b_eps, rstd_b, rstd_b_made)

            def powers_of_e():
                pool.wait_ge(vecs_made, 2)
                pool.tensor_tensor(sc[:, 0:1], e_base[:, :], vec(V_LOG_STEP), ALU.pow).then_inc(dt_raised, 1)
                pool.wait_ge(re_dt_made, 1)
                pool.tensor_tensor(sc[:, 4:5], e_base[:, :], sc[:, 3:4], ALU.pow).then_inc(mag_raised, 1)

            def low_u(g):
                for d in range(ND):
                    pool.wait_ge(u_high, g * ND + d + 1)
                    pool.tensor_tensor(ul[:, d, :], u[:, d, :], uh[:, d, :].bitcast(F32), ALU.subtract)\
                        .then_inc(u_low, 1)

            def low_weights(n):
                flat = [a[:, :, :].rearrange("p a b -> p (a b)") for a in ((w1, w1h, w1l), (h, w2h, w2l))[n]]
                for m in range(4):
                    full, high, low = (a[:, m * 512:(m + 1) * 512] for a in flat)
                    pool.wait_ge(w_high, 4 * n + m + 1)
                    pool.tensor_tensor(low, full, high.bitcast(F32), ALU.subtract).then_inc(w_low, 1)

            def low_h(k, f):
                if not has(k, 2):
                    return
                i = (k - 2) * NF + f
                pool.wait_ge(h_high, i + 1)
                if not (is_tick(k, 2) and f < HS):
                    pool.wait_ge(f2_done, i + 1 - HS)
                pool.tensor_tensor(hl[:, f % HS, :], h[:, f % HS, :], hh[:, f % HS, :].bitcast(F32),
                                   ALU.subtract).then_inc(h_low, 1)

            def tick(k):
                if is_tick(k, 0):
                    pool.wait_ge(vec_consts, VEC_CONSTS)
                    powers_of_e()
                    rstd_of_x(0)
                    low_u(0)
                    rstd_of_x(1)
                    low_weights(0)
                    return
                low_h(k, 0)
                low_h(k, 1)
                if has(k, 0):
                    low_u(k)
                low_h(k, 2)
                low_h(k, 3)
                if has(k, 1):
                    rstd_of_y1(k - 1)
                low_h(k, 4)
                if is_tick(k, 1):
                    low_weights(1)
                low_h(k, 5)
                low_h(k, 6)
                low_h(k, 7)
                if has(k, -1):
                    rstd_of_x(k + 1)

            run(pool, tick, NG + 1)

        @block.vector
        def _(dve):
            n_steps = [0]

            def step(ins):
                n_steps[0] += 1
                ins.then_inc(own_step, 1)

            def own():
                dve.wait_ge(own_step, n_steps[0])

            def carry(scratch):
                dve.tensor_copy(scratch[:, :], sign[:, :])

            def norm_stats(g, stats, mv, done):
                for n in range(NT):
                    dve.bn_stats(stats[:, n, :], rows(g)[:, n, :]).then_inc(done, 1)
                dve.wait_ge(done, g * (2 * NT) + NT)
                carry(carried[1])
                for n in range(NT):
                    dve.bn_aggr(mv[:, n, :], stats[:, n, :]).then_inc(done, 1)

            def normalise(g, dst, mv, r, done):
                for n in range(NT):
                    dve.tensor_scalar(dst[:, n, :], rows(g)[:, n, :], mv[:, n, 0:1], r[:, n:n + 1],
                                      ALU.subtract, ALU.mult).then_inc(done, 1)

            def normalise_x(g):
                dve.wait_ge(rstd_a_made, g + 1)
                normalise(g, xn, mv_a, rstd_a, xn_made)

            def high_u(g):
                for d in range(ND):
                    dve.wait_ge(u_made, g * (ND * SEQ) + SEQ * (d + 1))
                    dve.tensor_copy(uh[:, d, :], u[:, d, :]).then_inc(u_high, 1)

            def add_to_rows(g, ps, done):
                for n in range(2):
                    half = rows(g)[:, 2 * n:2 * n + 2, :]
                    dve.tensor_tensor(half, half, ps[:, n, :].rearrange("p (j d) -> p j d", d=D),
                                      ALU.add).then_inc(done, 1)

            wide = lambda table: table[:, :].unsqueeze(1).to_broadcast([P, SEQ, L])
            by_seq = lambda ap: ap.rearrange("p (s l) -> p s l", l=L)

            def rotate(g):
                dve.wait_ge(bu_swapped, g * 2 + 2)
                dve.tensor_tensor(by_seq(rot_c[:, :]), by_seq(ps_p[:, 0, :]), wide(cos_t), ALU.mult).then_inc(rotated, 1)
                dve.tensor_tensor(by_seq(rot_s[:, :]), by_seq(bu_sw[:, :]), wide(sin_t), ALU.mult).then_inc(rotated, 1)
                dve.wait_ge(rotated, g * 3 + 2)
                dve.tensor_tensor(drive[:, :], rot_c[:, :], rot_s[:, :], ALU.add).then_inc(rotated, 1)

            def scan(g):
                dve.wait_ge(rotated, g * 3 + 3)
                for n in range(SEQ):
                    dve.tensor_tensor_scan(seq(z, n), decay[:, :], seq(drive, n), 0.0,
                                           ALU.mult, ALU.add).then_inc(scanned, 1)

            def make_state(g):
                dve.wait_ge(scanned, g * SEQ + SEQ)
                dve.tensor_tensor(by_seq(back_c[:, :]), by_seq(z[:, :]), wide(cos_t), ALU.mult).then_inc(rotated_back, 1)
                dve.wait_ge(z_swapped, g * 2 + 2)
                dve.tensor_tensor(by_seq(back_s[:, :]), by_seq(z_sw[:, :]), wide(sin_t), ALU.mult)\
                   .then_inc(rotated_back, 1)
                dve.wait_ge(rotated_back, g * 2 + 2)
                dve.tensor_tensor(state[:, :], back_c[:, :], back_s[:, :], ALU.subtract).then_inc(state_made, 1)
                dve.wait_ge(state_made, g + 1)
                dve.tensor_copy(state_h[:, :], state[:, :]).then_inc(state_high, 1)
                dve.wait_ge(state_high, g + 1)
                dve.tensor_tensor(state_l[:, :], state[:, :], state_h[:, :].bitcast(F32), ALU.subtract)\
                   .then_inc(state_low, 1)

            def add_skip(g):
                dve.wait_ge(a_summed, g + 1)
                for d in range(ND):
                    dve.scalar_tensor_tensor(out=a_sum[:, d, :], in0=u[:, d, :], scalar=vec(V_DD + d),
                                             in1=ps_p[:, d, :], op0=ALU.mult, op1=ALU.add).then_inc(a_sum_made, 1)

            def add_gated(g):
                dve.wait_ge(a_turned, g + 1)
                add_to_rows(g, ps_q, y1_made)
                dve.wait_ge(y1_made, g * 2 + 2)
                carry(carried[0])
                norm_stats(g, stats_b, mv_b, stats_b_made)

            def make_v(g, v_free):
                dve.wait_ge(yn_turned, g + 1)
                for n in range(SEQ):
                    dve.tensor_scalar(seq(v[:, 1], n), seq(ps_q[:, 1], n), at_batch(scale_v, 1, g, n),
                                      at_batch(shift_v, 1, g, n), ALU.mult, ALU.add).then_inc(v_made_dve, 1)
                if v_free is not None:
                    dve.wait_ge(f1_done, v_free)
                for d, made in ((1, v_made_dve), (0, v_made_act)):
                    dve.wait_ge(made, g * SEQ + SEQ)
                    dve.tensor_copy(vh[:, d, :], v[:, d, :]).then_inc(v_high, 1)
                for n, d in enumerate((1, 0)):
                    dve.wait_ge(v_high, g * ND + n + 1)
                    dve.tensor_tensor(vl[:, d, :], v[:, d, :], vh[:, d, :].bitcast(F32), ALU.subtract)\
                       .then_inc(v_low, 1)

            part = lambda ct: mod[:, ct:ct + ND, :]

            def add_bias(first, last, bank):
                step(dve.tensor_tensor(
                    mod[:, first:last, :], ps_ff[:, bank, first * NB:last * NB].rearrange("p (c b) -> p c b", b=NB),
                    vecs[:, V_BM + first:V_BM + last].unsqueeze(2).to_broadcast([P, last - first, NB]), ALU.add))
                own()

            def set_up():
                c = lambda n: sc[:, n:n + 1]
                lam_re, lam_im = vec(V_LAM_RE), vec(V_LAM_IM)
                dve.memset(sign[HIGH, :], 1.0).then_inc(vec_consts, 1)
                dve.memset(sign[LOW, :], -1.0).then_inc(vec_consts, 1)
                dve.memset(ln_eps[:, :], LN_EPS).then_inc(vec_consts, 1)
                dve.memset(minus_half[:, :], -0.5).then_inc(vec_consts, 1)
                dve.memset(e_base[:, :], E_BASE).then_inc(vec_consts, 1)
                dve.wait_ge(vec_consts, VEC_CONSTS)
                dve.wait_ge(vecs_turned, 1)
                dve.tensor_copy(vecs[:, 0:NV1], ps_p[:, 0, 0:NV1]).then_inc(vecs_made, 1)
                dve.tensor_copy(t_cols[:, :, :], ps_p[:, 1, 0:ND * NB].rearrange("p (k b) -> p k b", b=NB))\
                   .then_inc(vecs_made, 1)
                dve.wait_ge(vecs_made, 2)
                step(dve.tensor_scalar(c(1), vec(V_LOG_STEP), E_REST, 1.0, ALU.mult, ALU.add))
                own()
                dve.wait_ge(dt_raised, 1)
                step(dve.tensor_tensor(c(2), c(0), c(1), ALU.mult))
                own()
                dve.tensor_tensor(c(3), lam_re, c(2), ALU.mult).then_inc(re_dt_made, 1)
                step(dve.tensor_tensor(c(5), lam_im, c(2), ALU.mult))
                own()
                step(dve.tensor_scalar(c(6), c(5), INV_TWO_PI, ROUND_TO_256TH, ALU.mult, ALU.add))
                own()
                step(dve.tensor_scalar(c(7), c(6), -ROUND_TO_256TH, None, ALU.add))
                own()
                dve.wait_ge(x_loaded[0], 16)
                norm_stats(0, stats_a, mv_a, stats_a_made)
                step(dve.tensor_scalar(turn_f[:, :], steps[:, :], c(7), None, ALU.mult))
                step(dve.scalar_tensor_tensor(out=c(8), in0=c(7), scalar=-TWO_PI_A, in1=c(5), op0=ALU.mult, op1=ALU.add))
                own()
                step(dve.tensor_scalar(turns_w[:, 0, :], turn_f[:, :], ROUND_TO_1, -ROUND_TO_1, ALU.add, ALU.add))
                step(dve.scalar_tensor_tensor(out=c(9), in0=c(7), scalar=-TWO_PI_B, in1=c(8), op0=ALU.mult, op1=ALU.add))
                own()
                step(dve.tensor_tensor(turn_c[:, :], turn_f[:, :], turns_w[:, 0, :], ALU.subtract))
                step(dve.scalar_tensor_tensor(out=c(10), in0=c(7), scalar=-TWO_PI_C, in1=c(9), op0=ALU.mult, op1=ALU.add))
                own()
                step(dve.tensor_scalar(c(11), c(10), INV_TWO_PI, None, ALU.mult))
                own()
                normalise_x(0)
                step(dve.scalar_tensor_tensor(out=turns[:, 0, :], in0=steps[:, :], scalar=c(11), in1=turn_c[:, :],
                                              op0=ALU.mult, op1=ALU.add))
                own()
                step(dve.tensor_scalar(turns[:, 1, :], turns[:, 0, :], 0.25, None, ALU.add))
                own()
                step(dve.tensor_scalar(turns_w[:, :, :], turns[:, :, :], ROUND_TO_1, -ROUND_TO_1, ALU.add, ALU.add))
                own()
                dve.tensor_tensor(turns_r[:, :, :], turns[:, :, :], turns_w[:, :, :], ALU.subtract).then_inc(turns_made, 1)
                dve.wait_ge(mod_a_summed, 1)
                add_bias(0, NA, 0)
                dve.tensor_scalar(scale_a[:, :, :], part(SCALE_A), 1.0, None, ALU.add).then_inc(mod_a_made, 1)
                step(dve.tensor_scalar(c(13), c(3), E_REST, 1.0, ALU.mult, ALU.add))
                step(dve.tensor_tensor(c(15), lam_re, lam_re, ALU.mult))
                own()
                dve.wait_ge(mag_raised, 1)
                step(dve.tensor_tensor(c(12), c(4), c(13), ALU.mult))
                step(dve.scalar_tensor_tensor(out=c(16), in0=lam_im, scalar=lam_im, in1=c(15), op0=ALU.mult, op1=ALU.add))
                own()
                step(dve.tensor_scalar(decay[:, :], steps[:, :], 0.0, c(12), ALU.mult, ALU.add))
                step(dve.reciprocal(c(17), c(16)))
                dve.wait_ge(trig_made, 2)
                step(dve.tensor_scalar(c(14), sin_raw[:, 1:2], c(12), None, ALU.mult))
                step(dve.tensor_scalar(c(18), cos_t[:, 1:2], c(12), -1.0, ALU.mult, ALU.add))
                own()
                step(dve.tensor_tensor(c(19), c(14), lam_im, ALU.mult))
                step(dve.tensor_tensor(c(21), c(18), lam_im, ALU.mult))
                own()
                step(dve.scalar_tensor_tensor(out=c(22), in0=c(14), scalar=lam_re, in1=c(21), op0=ALU.mult,
                                              op1=ALU.subtract))
                step(dve.scalar_tensor_tensor(out=c(20), in0=c(18), scalar=lam_re, in1=c(19), op0=ALU.mult, op1=ALU.add))
                own()
                step(dve.tensor_scalar(c(23), c(22), c(17), sign[:, :], ALU.mult, ALU.mult))
                step(dve.tensor_tensor(c(24), c(20), c(17), ALU.mult))
                own()
                dve.wait_ge(bc_loaded, 16 * N_BC_LOADS)
                step(dve.tensor_scalar(b_tmp[:, :], b_second[:, :], c(23), None, ALU.mult))
                own()
                dve.scalar_tensor_tensor(out=b_bar[:, :], in0=b_first[:, :], scalar=c(24), in1=b_tmp[:, :],
                                         op0=ALU.mult, op1=ALU.subtract).then_inc(b_bar_made, 1)
                step(dve.tensor_scalar(sin_t[:, :], sin_raw[:, :], sign[:, :], None, ALU.mult))
                high_u(0)
                dve.wait_ge(b_turned, 1)
                step(dve.tensor_copy(bT[:, :, :], ps_q[:, 0, 0:D].rearrange("p (k d) -> p k d", d=P)))
                own()
                dve.tensor_copy(bTh[:, :, :], bT[:, :, :]).then_inc(b_parts, 1)
                dve.wait_ge(b_parts, 1)
                dve.tensor_tensor(bTl[:, :, :], bT[:, :, :], bTh[:, :, :].bitcast(F32), ALU.subtract).then_inc(b_parts, 1)
                step(dve.tensor_scalar(c(25), sign[:, :], 2.0, None, ALU.mult))
                own()
                dve.wait_ge(c_turned, 1)
                step(dve.tensor_scalar(cT[:, :, :], ps_q[:, 1, 0:D].rearrange("p (k d) -> p k d", d=P),
                                       c(25), None, ALU.mult))
                own()
                dve.tensor_copy(cTh[:, :, :], cT[:, :, :]).then_inc(c_parts, 1)
                dve.wait_ge(c_parts, 1)
                dve.tensor_tensor(cTl[:, :, :], cT[:, :, :], cTh[:, :, :].bitcast(F32), ALU.subtract).then_inc(c_parts, 1)
                dve.tensor_copy(vecs[:, NV1:], ps_q[:, 1, D:D + NV2]).then_inc(vecs2_made, 1)
                dve.wait_ge(vecs2_made, 1)

            def set_up_rest():
                dve.wait_ge(mod_summed, 1)
                add_bias(NA, NM + NCC, 1)
                step(dve.tensor_scalar(scale_f1[:, :, :], part(SCALE_F), 1.0, None, ALU.add))
                own()
                step(dve.tensor_tensor(shift_v1[:, :, :], part(SHIFT_C), scale_f1[:, :, :], ALU.mult))
                own()
                dve.scalar_tensor_tensor(out=scale_v[:, :, :], in0=part(SCALE_C), scalar=1.0, in1=scale_f1[:, :, :],
                                         op0=ALU.add, op1=ALU.mult).then_inc(mod_made, 1)
                dve.tensor_tensor(shift_v[:, :, :], shift_v1[:, :, :], part(SHIFT_F), ALU.add).then_inc(mod_made, 1)
                dve.tensor_tensor(gate_b2[:, :, :], part(GATE_F),
                                  vecs[:, V_B2:V_B2 + ND].unsqueeze(2).to_broadcast([P, ND, NB]), ALU.mult)\
                   .then_inc(mod_made, 1)
                dve.wait_ge(mod_made, 3)

            def tick(k):
                a, b, c = k, k - 1, k - 2
                if is_tick(k, 0):
                    set_up()
                    dve.wait_ge(x_loaded[1], 16)
                    norm_stats(1, stats_a, mv_a, stats_a_made)
                    rotate(0)
                    scan(0)
                    make_state(0)
                    normalise_x(1)
                    set_up_rest()
                    return
                if has(k, 1):
                    add_skip(b)
                if has(k, 3):
                    dve.wait_ge(ff_turned, c)
                    add_to_rows(c - 1, ps_q, out_made)
                if has(k, 0):
                    high_u(a)
                if has(k, 1):
                    add_gated(b)
                if has(k, 0) and not is_tick(k, 1):
                    rotate(a)
                    scan(a)
                if has(k, 1):
                    dve.wait_ge(rstd_b_made, b + 1)
                    normalise(b, yn, mv_b, rstd_b, yn_made)
                if is_tick(k, 1):
                    rotate(a)
                    scan(a)
                    make_v(b, None)
                if has(k, 0):
                    make_state(a)
                if is_tick(k, 1):
                    dve.wait_ge(x_loaded[2], 16 * (NG - 2))
                if has(k, -1):
                    norm_stats(k + 1, stats_a, mv_a, stats_a_made)
                if has(k, 1) and not is_tick(k, 1):
                    make_v(b, c * NF + NF if has(k, 2) else None)
                if has(k, -1):
                    normalise_x(k + 1)

            run(dve, tick, NG + 2)

        @block.scalar
        def _(act):
            def gelu(k, f):
                if not has(k, 2):
                    return
                i = (k - 2) * NF + f
                if is_tick(k, 2) and f == 0:
                    act.wait_ge(w_low, 8)
                act.wait_ge(f1_done, i + 1)
                if not (is_tick(k, 2) and f < HS):
                    act.wait_ge(h_low, i + 1 - HS)
                    act.wait_ge(f2_done, i + 1 - HS)
                act.activation(h[:, f % HS, :], ps_h[:, f % 2, :], ACT.Gelu_apprx_tanh, bias=vec(V_B1 + f))\
                   .then_inc(h_made, 1)
                act.activation(hh[:, f % HS, :], ps_h[:, f % 2, :], ACT.Gelu_apprx_tanh, bias=vec(V_B1 + f))\
                   .then_inc(h_high, 1)

            def swap_halves(dst, src, done):
                act.activation(dst[HIGH, :], src[LOW, :], ACT.Copy).then_inc(done, 1)
                act.activation(dst[LOW, :], src[HIGH, :], ACT.Copy).then_inc(done, 1)

            def make_u(g):
                act.wait_ge(xn_turned, g + 1)
                for d in range(ND):
                    for n in range(SEQ):
                        act.activation(seq(u[:, d], n), seq(ps_p[:, d], n), ACT.Identity,
                                       scale=at_batch(scale_a, d, g, n),
                                       bias=at_batch(mod, SHIFT_A + d, g, n)).then_inc(u_made, 1)

            def first_half_of_v(g):
                act.wait_ge(yn_turned, g + 1)
                for n in range(SEQ):
                    act.activation(seq(v[:, 0], n), seq(ps_q[:, 0], n), ACT.Identity,
                                   scale=at_batch(scale_v, 0, g, n), bias=at_batch(shift_v, 0, g, n)).then_inc(v_made_act, 1)

            def high_weights(n):
                act.wait_ge(w_loaded[n], 16)
                full = w1[:, :, :].rearrange("p a b -> p (a b)") if n == 0 else h[:, :, :].rearrange("p a b -> p (a b)")
                high = (w1h, w2h)[n][:, :, :].rearrange("p a b -> p (a b)")
                for m in range(4):
                    act.activation(high[:, m * 512:(m + 1) * 512], full[:, m * 512:(m + 1) * 512], ACT.Copy)\
                       .then_inc(w_high, 1)

            def tick(k):
                a, b, c = k, k - 1, k - 2
                if is_tick(k, 0):
                    act.preload_act_table(ACT.Sin)
                    act.wait_ge(turns_made, 1)
                    act.activation(sin_raw[:, :], turns_r[:, 0, :], ACT.Sin, scale=TWO_PI_BELOW).then_inc(trig_made, 1)
                    act.activation(cos_t[:, :], turns_r[:, 1, :], ACT.Sin, scale=TWO_PI_BELOW).then_inc(trig_made, 1)
                    act.preload_act_table(ACT.Gelu_apprx_tanh)
                    act.wait_ge(mod_a_made, 1)
                    make_u(a)
                    act.wait_ge(bu_summed, a + 1)
                    swap_halves(bu_sw, ps_p[:, 0, :], bu_swapped)
                    high_weights(0)
                    act.wait_ge(scanned, a * SEQ + SEQ)
                    swap_halves(z_sw, z, z_swapped)
                    high_weights(1)
                    act.wait_ge(mod_made, 3)
                    return
                if has(k, 3):
                    act.wait_ge(f2_done, c * NF)
                    for n in range(SEQ):
                        for d in range(ND):
                            act.activation(seq(ff[:, d], n), seq(ps_ff[:, d], n), ACT.Identity,
                                           scale=at_batch(mod, GATE_F + d, c - 1, n),
                                           bias=at_batch(gate_b2, d, c - 1, n)).then_inc(ff_made, 1)
                for d in range(ND):
                    if has(k, 1):
                        act.wait_ge(a_sum_made, b * ND + d + 1)
                        for n in range(SEQ):
                            act.activation(seq(a_gated[:, d], n), seq(a_sum[:, d], n), ACT.Copy,
                                           scale=at_batch(mod, GATE_A + d, b, n)).then_inc(a_gated_made, 1)
                    gelu(k, d)
                if has(k, 0):
                    make_u(a)
                gelu(k, 2)
                gelu(k, 3)
                gelu(k, 4)
                if has(k, 0):
                    act.wait_ge(bu_summed, a + 1)
                    swap_halves(bu_sw, ps_p[:, 0, :], bu_swapped)
                gelu(k, 5)
                if is_tick(k, 1):
                    first_half_of_v(b)
                if has(k, 0):
                    act.wait_ge(scanned, a * SEQ + SEQ)
                    swap_halves(z_sw, z, z_swapped)
                gelu(k, 6)
                gelu(k, 7)
                if has(k, 1) and not is_tick(k, 1):
                    first_half_of_v(b)

            run(act, tick, NG + 2)

        @block.tensor
        def _(pe):
            def split_product(dst, wh, wl, ah, al, start, stop):
                pe.matmul(dst, wl, ah, start=start, stop=False)
                pe.matmul(dst, wh, al, start=False, stop=False)
                return pe.matmul(dst, wh, ah, start=False, stop=stop)

            def f1(k, f):
                if not has(k, 2):
                    return
                c = k - 2
                i = c * NF + f
                if f == 0:
                    pe.wait_ge(v_low, c * ND + ND)
                    if is_tick(k, 2):
                        pe.wait_ge(w_low, 4)
                if not (is_tick(k, 2) and f < 2):
                    pe.wait_ge(h_high, i - 1)
                fs = slice(f * P, (f + 1) * P)
                for kt in range(ND):
                    last = split_product(ps_h[:, f % 2, :], w1h[:, kt, fs], w1l[:, kt, fs], vh[:, kt, :], vl[:, kt, :],
                                         kt == 0, kt == ND - 1)
                last.then_inc(f1_done, 1)

            def f2(k, f):
                if not has(k, 2):
                    return
                i = (k - 2) * NF + f
                if is_tick(k, 2) and f == 0:
                    pe.wait_ge(w_low, 8)
                pe.wait_ge(h_low, i + 1)
                for d in range(ND):
                    cs = slice(d * P, (d + 1) * P)
                    last = split_product(ps_ff[:, d, :], w2h[:, f, cs], w2l[:, f, cs], hh[:, f % HS, :], hl[:, f % HS, :],
                                         f == 0, f == NF - 1)
                last.then_inc(f2_done, 1)

            def turn_to_columns(dst, src, done):
                for d in range(ND):
                    for n in range(NT):
                        last = pe.transpose(dst[:, d, n * P:(n + 1) * P], src[:, n, d * P:(d + 1) * P], ident[:, :])
                last.then_inc(done, 1)

            def turn_to_rows(dst, src, done):
                for n in range(NT):
                    for d in range(ND):
                        last = pe.transpose(dst[:, n // 2, (n % 2) * D + d * P:(n % 2) * D + (d + 1) * P],
                                            src[:, d, n * P:(n + 1) * P], ident[:, :])
                last.then_inc(done, 1)

            def turn_x(g, pair_free):
                pe.wait_ge(xn_made, g * NT + NT)
                if pair_free is not None:
                    pe.wait_ge(a_sum_made, pair_free)
                turn_to_columns(ps_p, xn, xn_turned)

            def sum_drive(g):
                pe.wait_ge(u_low, g * ND + ND)
                for kt in range(ND):
                    last = split_product(ps_p[:, 0, :], bTh[:, kt, :], bTl[:, kt, :], uh[:, kt, :], ul[:, kt, :],
                                         kt == 0, kt == ND - 1)
                last.then_inc(bu_summed, 1)

            def modulate(tiles, bank, done):
                for ct in tiles:
                    w, m = (wm, ct) if ct < NM else (wc, ct - NM)
                    for kt in range(ND):
                        last = pe.matmul(ps_ff[:, bank, ct * NB:(ct + 1) * NB], w[:, kt, m * P:(m + 1) * P],
                                         t_cols[:, kt, :], start=(kt == 0), stop=(kt == ND - 1))
                if done is not None:
                    last.then_inc(done, 1)

            def sum_states(g):
                pe.wait_ge(state_low, g + 1)
                for d in range(ND):
                    last = split_product(ps_p[:, d, :], cTh[:, d, :], cTl[:, d, :], state_h[:, :], state_l[:, :],
                                         True, True)
                last.then_inc(a_summed, 1)

            def tick(k):
                a, b, c = k, k - 1, k - 2
                if is_tick(k, 0):
                    pe.wait_ge(pool_consts, POOL_CONSTS)
                    pe.wait_ge(vecs_loaded, 16 * N_VEC_LOADS)
                    pe.transpose(ps_p[:, 0, 0:NV1], vec_rows1[:, :], ident[0:NV1, 0:NV1])
                    for d in range(ND):
                        last = pe.transpose(ps_p[:, 1, d * NB:(d + 1) * NB], t_rows[:, d * P:(d + 1) * P],
                                            ident[0:NB, 0:NB])
                    last.then_inc(vecs_turned, 1)
                    pe.wait_ge(wa_loaded, 16)
                    pe.wait_ge(vecs_made, 2)
                    modulate(range(NA), 0, mod_a_summed)
                    turn_x(a, None)
                    pe.wait_ge(bc_loaded, 16 * N_BC_LOADS)
                    pe.wait_ge(vecs2_loaded, 16 * 4)
                    for d in range(ND):
                        pe.transpose(ps_q[:, 1, d * P:(d + 1) * P], c_rows[:, d, :], ident[:, :])
                    pe.transpose(ps_q[:, 1, D:D + NV2], vec_rows2[:, :], ident[0:NV2, 0:NV2]).then_inc(c_turned, 1)
                    pe.wait_ge(b_bar_made, 1)
                    for d in range(ND):
                        last = pe.transpose(ps_q[:, 0, d * P:(d + 1) * P], b_bar[:, d * P:(d + 1) * P], ident[:, :])
                    last.then_inc(b_turned, 1)
                    pe.wait_ge(wm_loaded, 32)
                    modulate(range(NA, NA + ND), 1, None)
                    pe.wait_ge(b_parts, 2)
                    sum_drive(a)
                    modulate(range(NA + ND, NM + NCC), 1, mod_summed)
                    pe.wait_ge(c_parts, 2)
                    pe.wait_ge(mod_made, 3)
                    return
                if is_tick(k, 2):
                    f1(k, 0)
                    f1(k, 1)
                    sum_states(b)
                else:
                    if has(k, 1):
                        sum_states(b)
                    f1(k, 0)
                    f1(k, 1)
                if has(k, 3):
                    pe.wait_ge(ff_made, c * (ND * SEQ))
                    if has(k, 2):
                        pe.wait_ge(v_low, b * ND)
                    else:
                        pe.wait_ge(out_made, (c - 1) * 2)
                    turn_to_rows(ps_q, ff, ff_turned)
                if has(k, 0):
                    turn_x(a, b * ND + ND)
                f1(k, 2)
                f2(k, 0)
                f1(k, 3)
                if has(k, 1):
                    pe.wait_ge(a_gated_made, b * (ND * SEQ) + ND * SEQ)
                    if has(k, 3):
                        pe.wait_ge(out_made, c * 2)
                    turn_to_rows(ps_q, a_gated, a_turned)
                f2(k, 1)
                if has(k, 0):
                    sum_drive(a)
                f1(k, 4)
                f2(k, 2)
                f1(k, 5)
                f2(k, 3)
                f1(k, 6)
                f2(k, 4)
                f1(k, 7)
                if has(k, 1):
                    pe.wait_ge(yn_made, b * NT + NT)
                    turn_to_columns(ps_q, yn, yn_turned)
                f2(k, 5)
                f2(k, 6)
                f2(k, 7)

            run(pe, tick, NG + 2)


_INS = ['x', 'cond_1024'] + ['L0_cond_' + n for n in (
    'Wm', 'bm', 'Lam_re', 'Lam_im', 'B_re', 'B_im', 'C_re', 'C_im', 'D_diag', 'log_step', 'Wc', 'bc', 'W1', 'b1', 'W2', 'b2')]


def kernel(**inputs):
    import numpy as np
    import concourse.bacc as bacc
    from concourse.bass_utils import run_bass_kernel_spmd

    nc = bacc.Bacc("TRN2", target_bir_lowering=False, num_devices=1)
    arrays, args = {}, []
    for name in _INS:
        a = np.ascontiguousarray(inputs[name])
        arrays["in_" + name] = a
        args.append(nc.dram_tensor("in_" + name, a.shape, mybir.dt.from_np(a.dtype), kind="ExternalInput").ap())
    shape = inputs["x"].shape
    args.append(nc.dram_tensor("out_y", shape, F32, kind="ExternalOutput").ap())
    cond_seq_kernel(nc, *args)
    r = run_bass_kernel_spmd(nc, [arrays], core_ids=[0])
    return r.results[0]["out_y"]
```

```python
from contextlib import ExitStack

import concourse.bass as bass
from concourse import mybir

F32 = mybir.dt.float32
F32R = mybir.dt.float32r
ALU = mybir.AluOpType
ACT = mybir.ActivationFunctionType

LN_EPS = 1e-5
P = 128
TWO_PI_A = 6.28125
TWO_PI_B = 0.0019350051879882812
TWO_PI_C = 3.019916050561733e-07
INV_TWO_PI = 0.15915494309189535
TWO_PI_BELOW = 6.283185005187988
ROUND_TO_1 = 12582912.0
ROUND_TO_256TH = 49152.0
E_BASE = 2.7182817459106445
E_REST = 3.0367860004432146e-08


def cond_seq_kernel(nc, x, t, Wm, bm, Lam_re, Lam_im, B_re, B_im, C_re, C_im, D_diag, log_step,
                    Wc, bc, W1, b1, W2, b2, out):
    NB, L, D = x.shape
    S = Lam_re.shape[0]
    F = W1.shape[1]
    SEQ = 2
    GT = SEQ * L
    NG = NB // SEQ
    NT = GT // P
    TS = L // P
    ND = D // P
    NF = F // P
    NM = Wm.shape[1] // P
    NCC = Wc.shape[1] // P
    HS = 4
    assert 2 * S == P and GT == 512 and NG >= 6

    with ExitStack() as ctx:
        def sb(name, shape, dt=F32):
            return ctx.enter_context(nc.sbuf_tensor(name, shape, dt))

        def sem(name):
            return ctx.enter_context(nc.semaphore(name))

        ps_h = ctx.enter_context(nc.psum_tensor("ps_h", [P, 2, GT], F32))
        ps_ff = ctx.enter_context(nc.psum_tensor("ps_ff", [P, ND, GT], F32))
        ps_p = ctx.enter_context(nc.psum_tensor("ps_p", [P, SEQ, GT], F32))
        ps_q = ctx.enter_context(nc.psum_tensor("ps_q", [P, SEQ, GT], F32))

        ident = sb("ident", [P, P])
        steps = sb("steps", [P, L])
        sign = sb("sign", [P, 1])
        twice_sign = sb("twice_sign", [P, 1])
        two_pi = sb("two_pi", [P, 1])
        ln_eps = sb("ln_eps", [P, NT])
        minus_half = sb("minus_half", [P, NT])
        e_base = sb("e_base", [P, 1])
        c_rows = sb("c_rows", [P, ND, P])
        b_first = sb("b_first", [P, D])
        b_second = sb("b_second", [P, D])
        w1 = sb("w1", [P, ND, F])
        w1h, w1l = sb("w1h", [P, ND, F], F32R), sb("w1l", [P, ND, F], F32R)
        w2h, w2l = sb("w2h", [P, NF, D], F32R), sb("w2l", [P, NF, D], F32R)
        wm = sb("wm", [P, ND, NM * P])
        wc = sb("wc", [P, ND, NCC * P])
        NV1, NV2 = 3 + NM, NCC + ND + ND + NF
        vec_rows1, vec_rows2 = sb("vec_rows1", [NV1, P]), sb("vec_rows2", [NV2, P])
        vecs = sb("vecs", [P, NV1 + NV2])
        t_rows = sb("t_rows", [NB, D])
        t_cols = sb("t_cols", [P, ND, NB])
        mod = sb("mod", [P, NM + NCC, NB])
        scale_a = sb("scale_a", [P, ND, NB])
        scale_c1 = sb("scale_c1", [P, ND, NB])
        scale_f1 = sb("scale_f1", [P, ND, NB])
        scale_v = sb("scale_v", [P, ND, NB])
        shift_v1 = sb("shift_v1", [P, ND, NB])
        shift_v = sb("shift_v", [P, ND, NB])
        gate_b2 = sb("gate_b2", [P, ND, NB])
        sc = sb("sc", [P, 32])
        turn_f = sb("turn_f", [P, L])
        turn_c = sb("turn_c", [P, L])
        turns = sb("turns", [P, 2, L])
        turns_w = sb("turns_w", [P, 2, L])
        turns_r = sb("turns_r", [P, 2, L])
        cos_t = sb("cos_t", [P, L])
        trig1 = sb("trig1", [P, 2, 1])
        sin_t = sb("sin_t", [P, L])
        decay = sb("decay", [P, L])
        b_bar = sb("b_bar", [P, D])
        b_tmp = sb("b_tmp", [P, D])
        bT = sb("bT", [P, ND, P])
        bTh, bTl = sb("bTh", [P, ND, P], F32R), sb("bTl", [P, ND, P], F32R)
        cT = sb("cT", [P, ND, P])
        cTh, cTl = sb("cTh", [P, ND, P], F32R), sb("cTl", [P, ND, P], F32R)
        carried = [sb(f"carried{n}", [P, 1]) for n in range(2)]

        xs = sb("xs", [P, NG, NT, D])
        stats_a, stats_b = sb("stats_a", [P, NT, 6]), sb("stats_b", [P, NT, 6])
        mv_a, mv_b = sb("mv_a", [P, NT, 2]), sb("mv_b", [P, NT, 2])
        var_a, var_b = sb("var_a", [P, NT]), sb("var_b", [P, NT])
        rstd_a, rstd_b = sb("rstd_a", [P, NT]), sb("rstd_b", [P, NT])
        xn = sb("xn", [P, NT, D])
        yn = sb("yn", [P, NT, D])
        u = sb("u", [P, ND, GT])
        uh, ul = sb("uh", [P, ND, GT], F32R), sb("ul", [P, ND, GT], F32R)
        bu_sw = sb("bu_sw", [P, GT])
        rot_c = sb("rot_c", [P, GT])
        rot_s = sb("rot_s", [P, GT])
        drive = sb("drive", [P, GT])
        z = sb("z", [P, GT])
        z_sw = sb("z_sw", [P, GT])
        back_c = sb("back_c", [P, GT])
        back_s = sb("back_s", [P, GT])
        state = sb("state", [P, GT])
        state_h, state_l = sb("state_h", [P, GT], F32R), sb("state_l", [P, GT], F32R)
        a_sum = sb("a_sum", [P, ND, GT])
        a_gated = sb("a_gated", [P, ND, GT])
        v = sb("v", [P, ND, GT])
        vh, vl = sb("vh", [P, ND, GT], F32R), sb("vl", [P, ND, GT], F32R)
        h = sb("h", [P, HS, GT])
        w2 = h[:, :, :].rearrange("p s (k n) -> p (s k) n", n=D)
        hh, hl = sb("hh", [P, HS, GT], F32R), sb("hl", [P, HS, GT], F32R)
        ff = sb("ff", [P, ND, GT])

        x_loaded = [sem("x0_loaded"), sem("x1_loaded"), sem("x2_loaded"), sem("x_rest_loaded")]
        vecs_loaded = sem("vecs_loaded")
        vecs2_loaded = sem("vecs2_loaded")
        bc_loaded = sem("bc_loaded")
        wa_loaded = sem("wa_loaded")
        wb_loaded = sem("wb_loaded")
        wm_loaded = sem("wm_loaded")
        wc_loaded = sem("wc_loaded")
        w_loaded = [sem("w1_loaded"), sem("w2_loaded")]
        stored = sem("stored")
        pool_consts = sem("pool_consts")
        vec_consts = sem("vec_consts")
        own_step = sem("own_step")
        vecs_turned = sem("vecs_turned")
        vecs_made = sem("vecs_made")
        dt_raised = sem("dt_raised")
        re_dt_made = sem("re_dt_made")
        mag_raised = sem("mag_raised")
        turns_made = sem("turns_made")
        trig1_made = sem("trig1_made")
        trig_made = sem("trig_made")
        mod_a_summed = sem("mod_a_summed")
        gate_a_summed = sem("gate_a_summed")
        gate_a_made = sem("gate_a_made")
        mod_a_made = sem("mod_a_made")
        b_bar_made = sem("b_bar_made")
        b_turned = sem("b_turned")
        b_high = sem("b_high")
        b_low = sem("b_low")
        c_turned = sem("c_turned")
        c_high = sem("c_high")
        c_low = sem("c_low")
        mod_summed = sem("mod_summed")
        mod_rest_made = sem("mod_rest_made")
        mod_made = sem("mod_made")
        vecs2_made = sem("vecs2_made")
        w_high = sem("w_high")
        w_low = sem("w_low")
        stats_a_made = sem("stats_a_made")
        var_a_eps = sem("var_a_eps")
        rstd_a_made = sem("rstd_a_made")
        xn_made = sem("xn_made")
        xn_turned = sem("xn_turned")
        u_made = sem("u_made")
        u_high = sem("u_high")
        u_high_early = sem("u_high_early")
        u_low = sem("u_low")
        bu_summed = sem("bu_summed")
        bu_swapped = sem("bu_swapped")
        rotated = sem("rotated")
        scanned = sem("scanned")
        z_swapped = sem("z_swapped")
        rotated_back = sem("rotated_back")
        state_made = sem("state_made")
        state_high = sem("state_high")
        state_low = sem("state_low")
        a_summed = sem("a_summed")
        a_sum_made = sem("a_sum_made")
        a_gated_made = sem("a_gated_made")
        a_turned = sem("a_turned")
        y1_made = sem("y1_made")
        stats_b_made = sem("stats_b_made")
        var_b_eps = sem("var_b_eps")
        rstd_b_made = sem("rstd_b_made")
        yn_made = sem("yn_made")
        yn_turned = sem("yn_turned")
        v_made_act = sem("v_made_act")
        v_made_dve = sem("v_made_dve")
        v_high = sem("v_high")
        v_low = sem("v_low")
        f1_done = sem("f1_done")
        h_made = sem("h_made")
        h_high = sem("h_high")
        h_low = sem("h_low")
        f2_done = sem("f2_done")
        ff_made = sem("ff_made")
        last_ff_made = sem("last_ff_made")
        ff_turned = sem("ff_turned")
        out_made = sem("out_made")

        x_rows = x.rearrange("(g h) (j p) d -> g p (h j) d", h=SEQ, p=P)
        out_rows = out.rearrange("(g h) (j p) d -> g p (h j) d", h=SEQ, p=P)
        HIGH, LOW = slice(0, S), slice(S, P)
        V_LAM_RE, V_LAM_IM, V_LOG_STEP, V_BM = range(4)
        V_BC = NV1
        V_DD, V_B2, V_B1 = range(V_BC + NCC, V_BC + NCC + 3 * ND, ND)
        vec = lambda r: vecs[:, r:r + 1]
        SHIFT_A, SCALE_A, GATE_A, SHIFT_F, SCALE_F, GATE_F = range(0, NM, ND)
        SCALE_C, SHIFT_C = range(NM, NM + NCC, ND)
        NA = 2 * ND
        N_VEC_LOADS, N_BC_LOADS = 5, 2 + 4
        POOL_CONSTS, VEC_CONSTS, MOD_STEPS = 3, 9, 6

        def seq(tile, n):
            return tile[..., n * L:(n + 1) * L]

        def bank(ps, n, d):
            return ps[:, n, d * L:(d + 1) * L]

        def at_batch(table, ct, g, n):
            return table[:, ct, bass.ds(g * SEQ + n, 1)]

        def rows(g):
            return xs[:, bass.ds(g, 1)].rearrange("p g n d -> p (g n) d")

        def part(ct):
            return mod[:, ct:ct + ND, :]

        def run(eng, fill, tick, last):
            fill()
            with eng.Fori(3, NG - 1) as k:
                tick(k)
            for k in range(NG - 1, last + 1):
                tick(k)

        def has(k, lag):
            return not isinstance(k, int) or 0 <= k - lag < NG

        block = ctx.enter_context(nc.Block())

        @block.sync
        def _(sp):
            def load_vec(rows_tile, r, a, done):
                a = a.rearrange("(r p) -> r p", p=P)
                sp.dma_start(rows_tile[r:r + a.shape[0], :], a).then_inc(done, 16)

            sp.dma_start(xs[:, 0], x_rows[0]).then_inc(x_loaded[0], 16)
            for r, a in ((V_LAM_RE, Lam_re), (V_LAM_IM, Lam_im), (V_LOG_STEP, log_step)):
                sp.dma_start(vec_rows1[r:r + 1, :].rearrange("o (h s) -> o h s", s=S),
                             a.rearrange("(o h s) -> o h s", o=1, h=1).to_broadcast([1, 2, S])).then_inc(vecs_loaded, 16)
            sp.dma_start(t_rows[:, :], t).then_inc(vecs_loaded, 16)
            load_vec(vec_rows1, V_BM, bm, vecs_loaded)
            wm_cols = Wm.rearrange("(k p) n -> p k n", p=P)
            sp.dma_start(wm[:, :, 0:NA * P], wm_cols[:, :, 0:NA * P]).then_inc(wa_loaded, 16)
            for half, first, second in ((HIGH, B_re, B_im), (LOW, B_im, B_re)):
                sp.dma_start(b_first[half, :], first).then_inc(bc_loaded, 16)
                sp.dma_start(b_second[half, :], second).then_inc(bc_loaded, 16)
            sp.dma_start(wm[:, :, NA * P:2 * NA * P], wm_cols[:, :, NA * P:2 * NA * P]).then_inc(wb_loaded, 16)
            sp.dma_start(c_rows[:, :, 0:S], C_re.rearrange("(k p) s -> p k s", p=P)).then_inc(bc_loaded, 16)
            sp.dma_start(c_rows[:, :, S:P], C_im.rearrange("(k p) s -> p k s", p=P)).then_inc(bc_loaded, 16)
            for v_col, a in ((V_BC, bc), (V_DD, D_diag), (V_B2, b2), (V_B1, b1)):
                load_vec(vec_rows2, v_col - NV1, a, vecs2_loaded)
            sp.dma_start(wm[:, :, 2 * NA * P:], wm_cols[:, :, 2 * NA * P:]).then_inc(wm_loaded, 16)
            sp.dma_start(wc[:, :, :], Wc.rearrange("(k p) n -> p k n", p=P)).then_inc(wc_loaded, 16)
            sp.dma_start(xs[:, 1], x_rows[1]).then_inc(x_loaded[1], 16)
            sp.dma_start(w1[:, :, :], W1.rearrange("(k p) n -> p k n", p=P)).then_inc(w_loaded[0], 16)
            sp.dma_start(w2, W2.rearrange("(k p) n -> p k n", p=P)).then_inc(w_loaded[1], 16)
            for g in range(2, NG):
                sp.dma_start(xs[:, g], x_rows[g]).then_inc(x_loaded[min(g, 3)], 16)
            with sp.Fori(0, NG) as g:
                for n in range(SEQ):
                    half = slice(TS * n, TS * (n + 1))
                    sp.wait_ge(out_made, g * SEQ + n + 1)
                    sp.dma_start(out_rows[bass.ds(g, 1), :, half, :].rearrange("g p n d -> (g p) n d"),
                                 rows(g)[:, half, :]).then_inc(stored, 16)
            sp.wait_ge(stored, 16 * SEQ * NG)

        @block.gpsimd
        def _(pool):
            pool.iota(steps[:, :], [[1, L]], base=0, channel_multiplier=0,
                      allow_small_or_imprecise_dtypes=True).then_inc(pool_consts, 1)
            pool.wait_ge(pool_consts, 1)
            pool.memset(ident[:, :], 0.0).then_inc(pool_consts, 1)
            pool.wait_ge(pool_consts, 2)
            pool.affine_select(ident[:, :], ident[:, :], pattern=[[-1, P]], compare_op=ALU.not_equal,
                               fill=1.0, base=0, channel_multiplier=1).then_inc(pool_consts, 1)

            def rstd(i, count, tiles, stats_sem, mv, var, eps_sem, r, r_sem):
                pool.wait_ge(stats_sem, i * count + count)
                pool.tensor_tensor(var[:, tiles], mv[:, tiles, 1], ln_eps[:, tiles], ALU.add).then_inc(eps_sem, 1)
                pool.wait_ge(eps_sem, i + 1)
                pool.tensor_tensor(r[:, tiles], var[:, tiles], minus_half[:, tiles], ALU.pow).then_inc(r_sem, 1)

            def rstd_of_x(g):
                rstd(g, 2 * NT, slice(0, NT), stats_a_made, mv_a, var_a, var_a_eps, rstd_a, rstd_a_made)

            def rstd_of_y1(g):
                for n in range(SEQ):
                    rstd(g * SEQ + n, 2 * TS, slice(n * TS, (n + 1) * TS), stats_b_made, mv_b, var_b, var_b_eps,
                         rstd_b, rstd_b_made)

            def low_u(g, made=u_high, before=None, ns=range(SEQ)):
                before = (g - 1) * SEQ if before is None else before
                for n in ns:
                    pool.wait_ge(made, before + (n + 1) * (ND if made is u_high_early else 1))
                    pool.tensor_tensor(seq(ul, n), seq(u, n), seq(uh, n).bitcast(F32), ALU.subtract).then_inc(u_low, 1)

            def make_modulation():
                pool.wait_ge(mod_rest_made, 1)
                pool.tensor_scalar(scale_f1[:, :, :], part(SCALE_F), 1.0, None, ALU.add).then_inc(mod_made, 1)
                pool.wait_ge(mod_made, 1)
                pool.tensor_scalar(scale_c1[:, :, :], part(SCALE_C), 1.0, None, ALU.add).then_inc(mod_made, 1)
                pool.wait_ge(mod_made, 2)
                pool.tensor_tensor(scale_v[:, :, :], scale_c1[:, :, :], scale_f1[:, :, :], ALU.mult).then_inc(mod_made, 1)
                pool.wait_ge(mod_made, 3)
                pool.tensor_tensor(shift_v1[:, :, :], part(SHIFT_C), scale_f1[:, :, :], ALU.mult).then_inc(mod_made, 1)
                pool.wait_ge(mod_made, 4)
                pool.tensor_tensor(shift_v[:, :, :], shift_v1[:, :, :], part(SHIFT_F), ALU.add).then_inc(mod_made, 1)
                pool.wait_ge(mod_made, 5)
                pool.tensor_tensor(gate_b2[:, :, :], part(GATE_F),
                                   vecs[:, V_B2:V_B2 + ND].unsqueeze(2).to_broadcast([P, ND, NB]), ALU.mult)\
                    .then_inc(mod_made, 1)

            def low_weights(n, chunks=range(4)):
                flat = [a[:, :, :].rearrange("p a b -> p (a b)") for a in ((w1, w1h, w1l), (h, w2h, w2l))[n]]
                for m in chunks:
                    full, high, low = (a[:, m * 512:(m + 1) * 512] for a in flat)
                    pool.wait_ge(w_high, 4 * n + m + 1)
                    pool.tensor_tensor(low, full, high.bitcast(F32), ALU.subtract).then_inc(w_low, 1)

            def low_h(c, f):
                i = c * NF + f
                pool.wait_ge(h_high, i + 1)
                if not (isinstance(c, int) and i < HS):
                    pool.wait_ge(f2_done, i + 1 - HS)
                pool.tensor_tensor(hl[:, f % HS, :], h[:, f % HS, :], hh[:, f % HS, :].bitcast(F32),
                                   ALU.subtract).then_inc(h_low, 1)

            def fill():
                pool.wait_ge(vec_consts, VEC_CONSTS)
                rstd_of_x(0)
                pool.wait_ge(vecs_made, 2)
                pool.tensor_tensor(sc[:, 0:1], e_base[:, :], vec(V_LOG_STEP), ALU.pow).then_inc(dt_raised, 1)
                pool.wait_ge(re_dt_made, 1)
                pool.tensor_tensor(sc[:, 4:5], e_base[:, :], sc[:, 3:4], ALU.pow).then_inc(mag_raised, 1)
                low_u(0, before=0, ns=[0])
                pool.wait_ge(b_high, 2)
                pool.tensor_tensor(bTl[:, :, :], bT[:, :, :], bTh[:, :, :].bitcast(F32), ALU.subtract).then_inc(b_low, 1)
                low_u(0, before=0, ns=[1])
                pool.wait_ge(c_high, 2)
                pool.tensor_tensor(cTl[:, :, :], cT[:, :, :], cTh[:, :, :].bitcast(F32), ALU.subtract).then_inc(c_low, 1)
                rstd_of_x(1)
                low_weights(0)
                make_modulation()
                low_weights(1, (0, 1))
                rstd_of_y1(0)
                low_u(1, u_high_early, 0)
                low_weights(1, (2, 3))
                low_h(0, 0)
                low_h(0, 1)
                rstd_of_x(2)
                low_h(0, 2)
                low_h(0, 3)
                low_h(0, 4)
                rstd_of_y1(1)
                low_u(2)
                low_h(0, 5)
                low_h(0, 6)
                low_h(0, 7)

            def tick(k):
                c = k - 2
                if has(k, 2):
                    low_h(c, 0)
                if has(k, 0):
                    rstd_of_x(k)
                low_h(c, 1)
                if has(k, 0):
                    low_u(k)
                low_h(c, 2)
                low_h(c, 3)
                if has(k, 1):
                    rstd_of_y1(k - 1)
                for f in range(4, NF):
                    low_h(c, f)

            run(pool, fill, tick, NG + 1)

        @block.vector
        def _(dve):
            n_steps = [0]

            def step(ins):
                n_steps[0] += 1
                ins.then_inc(own_step, 1)

            def own():
                dve.wait_ge(own_step, n_steps[0])

            def carry(scratch):
                dve.tensor_copy(scratch[:, :], sign[:, :])

            def norm_stats(i, count, group_tiles, tiles, stats, mv, done):
                for n in tiles:
                    dve.bn_stats(stats[:, n, :], group_tiles[:, n, :]).then_inc(done, 1)
                dve.wait_ge(done, i * (2 * count) + count)
                carry(carried[1])
                for n in tiles:
                    dve.bn_aggr(mv[:, n, :], stats[:, n, :]).then_inc(done, 1)

            def stats_of_x(g):
                norm_stats(g, NT, rows(g), range(NT), stats_a, mv_a, stats_a_made)

            def normalise_x(g):
                dve.wait_ge(rstd_a_made, g + 1)
                for n in range(NT):
                    dve.tensor_scalar(xn[:, n, :], rows(g)[:, n, :], mv_a[:, n, 0:1], rstd_a[:, n:n + 1],
                                      ALU.subtract, ALU.mult).then_inc(xn_made, 1)

            def normalise_y1(g, tiles=range(NT)):
                for n in tiles:
                    if n % TS == 0:
                        dve.wait_ge(rstd_b_made, g * SEQ + n // TS + 1)
                    dve.tensor_scalar(yn[:, n, :], rows(g)[:, n, :], mv_b[:, n, 0:1], rstd_b[:, n:n + 1],
                                      ALU.subtract, ALU.mult).then_inc(yn_made, 1)

            def high_u(g):
                for n in range(SEQ):
                    dve.wait_ge(u_made, (g * SEQ + n + 1) * ND)
                    dve.tensor_copy(seq(uh, n), seq(u, n)).then_inc(u_high, 1)

            def add_to_rows(g, n, done):
                half = rows(g)[:, TS * n:TS * (n + 1), :]
                dve.tensor_tensor(half, half, ps_q[:, n, :].rearrange("p (j d) -> p j d", d=D), ALU.add).then_inc(done, 1)

            def rotate_and_scan(g, ns=range(SEQ)):
                for n in ns:
                    s = g * SEQ + n
                    dve.wait_ge(bu_swapped, s * 2 + 2)
                    dve.tensor_tensor(seq(rot_c, n), bank(ps_p, n, 0), cos_t[:, :], ALU.mult).then_inc(rotated, 1)
                    dve.tensor_tensor(seq(rot_s, n), seq(bu_sw, n), sin_t[:, :], ALU.mult).then_inc(rotated, 1)
                    dve.wait_ge(rotated, s * 3 + 2)
                    dve.tensor_tensor(seq(drive, n), seq(rot_c, n), seq(rot_s, n), ALU.add).then_inc(rotated, 1)
                    dve.wait_ge(rotated, s * 3 + 3)
                    dve.tensor_tensor_scan(seq(z, n), decay[:, :], seq(drive, n), 0.0,
                                           ALU.mult, ALU.add).then_inc(scanned, 1)

            def make_state(g):
                for n in range(SEQ):
                    s = g * SEQ + n
                    dve.wait_ge(scanned, s + 1)
                    dve.tensor_tensor(seq(back_c, n), seq(z, n), cos_t[:, :], ALU.mult).then_inc(rotated_back, 1)
                    dve.wait_ge(z_swapped, s * 2 + 2)
                    dve.tensor_tensor(seq(back_s, n), seq(z_sw, n), sin_t[:, :], ALU.mult).then_inc(rotated_back, 1)
                    dve.wait_ge(rotated_back, s * 2 + 2)
                    dve.tensor_tensor(seq(state, n), seq(back_c, n), seq(back_s, n), ALU.subtract).then_inc(state_made, 1)
                    dve.wait_ge(state_made, s + 1)
                    dve.tensor_copy(seq(state_h, n), seq(state, n)).then_inc(state_high, 1)
                    dve.wait_ge(state_high, s + 1)
                    dve.tensor_tensor(seq(state_l, n), seq(state, n), seq(state_h, n).bitcast(F32), ALU.subtract)\
                       .then_inc(state_low, 1)

            def add_skip(g, ns=range(SEQ)):
                for n in ns:
                    dve.wait_ge(a_summed, g * SEQ + n + 1)
                    for d in range(ND):
                        dve.scalar_tensor_tensor(out=seq(a_sum[:, d], n), in0=seq(u[:, d], n), scalar=vec(V_DD + d),
                                                 in1=bank(ps_p, n, d), op0=ALU.mult, op1=ALU.add).then_inc(a_sum_made, 1)

            def add_gated(g):
                for n in range(SEQ):
                    s = g * SEQ + n
                    dve.wait_ge(a_turned, s + 1)
                    add_to_rows(g, n, y1_made)
                    dve.wait_ge(y1_made, s + 1)
                    carry(carried[0])
                    norm_stats(s, TS, rows(g), range(n * TS, (n + 1) * TS), stats_b, mv_b, stats_b_made)

            def gate_last_ff(g):
                dve.wait_ge(f2_done, g * NF + NF)
                for n in range(SEQ):
                    dve.tensor_scalar(seq(ff[:, 1], n), seq(ps_ff[:, 1], n), at_batch(mod, GATE_F + 1, g, n),
                                      at_batch(gate_b2, 1, g, n), ALU.mult, ALU.add).then_inc(last_ff_made, 1)

            def add_ff(g):
                for n in range(SEQ):
                    dve.wait_ge(ff_turned, g * SEQ + n + 1)
                    add_to_rows(g, n, out_made)

            def make_v(g, v_free, order):
                if v_free is not None:
                    dve.wait_ge(f1_done, v_free)
                for i, n in enumerate(order):
                    s = g * SEQ + n
                    if n == 0:
                        dve.wait_ge(v_made_act, g * ND + ND)
                    else:
                        dve.wait_ge(yn_turned, s + 1)
                        for d in range(ND):
                            dve.tensor_scalar(seq(v[:, d], n), bank(ps_q, n, d), at_batch(scale_v, d, g, n),
                                              at_batch(shift_v, d, g, n), ALU.mult, ALU.add).then_inc(v_made_dve, 1)
                        dve.wait_ge(v_made_dve, g * ND + ND)
                    dve.tensor_copy(seq(vh, n), seq(v, n)).then_inc(v_high, 1)
                    dve.wait_ge(v_high, g * SEQ + i + 1)
                    dve.tensor_tensor(seq(vl, n), seq(v, n), seq(vh, n).bitcast(F32), ALU.subtract).then_inc(v_low, 1)

            def add_bias(first, last, ps):
                step(dve.tensor_tensor(
                    mod[:, first:last, :], ps[:, first * NB:last * NB].rearrange("p (c b) -> p c b", b=NB),
                    vecs[:, V_BM + first:V_BM + last].unsqueeze(2).to_broadcast([P, last - first, NB]), ALU.add))
                own()

            def set_up():
                c = lambda n: sc[:, n:n + 1]
                lam_re, lam_im = vec(V_LAM_RE), vec(V_LAM_IM)
                dve.memset(sign[HIGH, :], 1.0).then_inc(vec_consts, 1)
                dve.memset(sign[LOW, :], -1.0).then_inc(vec_consts, 1)
                dve.memset(ln_eps[:, :], LN_EPS).then_inc(vec_consts, 1)
                dve.memset(minus_half[:, :], -0.5).then_inc(vec_consts, 1)
                dve.memset(e_base[:, :], E_BASE).then_inc(vec_consts, 1)
                dve.memset(twice_sign[HIGH, :], 2.0).then_inc(vec_consts, 1)
                dve.memset(twice_sign[LOW, :], -2.0).then_inc(vec_consts, 1)
                dve.memset(two_pi[HIGH, :], TWO_PI_BELOW).then_inc(vec_consts, 1)
                dve.memset(two_pi[LOW, :], -TWO_PI_BELOW).then_inc(vec_consts, 1)
                dve.wait_ge(vec_consts, VEC_CONSTS)
                dve.wait_ge(x_loaded[0], 16)
                stats_of_x(0)
                dve.wait_ge(vecs_turned, 1)
                dve.tensor_copy(vecs[:, 0:NV1], ps_p[:, 0, 0:NV1]).then_inc(vecs_made, 1)
                dve.tensor_copy(t_cols[:, :, :], ps_p[:, 1, 0:ND * NB].rearrange("p (k b) -> p k b", b=NB))\
                   .then_inc(vecs_made, 1)
                dve.wait_ge(vecs_made, 2)
                step(dve.tensor_scalar(c(1), vec(V_LOG_STEP), E_REST, 1.0, ALU.mult, ALU.add))
                normalise_x(0)
                own()
                dve.wait_ge(dt_raised, 1)
                step(dve.tensor_tensor(c(2), c(0), c(1), ALU.mult))
                own()
                dve.tensor_tensor(c(3), lam_re, c(2), ALU.mult).then_inc(re_dt_made, 1)
                step(dve.tensor_tensor(c(5), lam_im, c(2), ALU.mult))
                own()
                step(dve.tensor_scalar(c(6), c(5), INV_TWO_PI, ROUND_TO_256TH, ALU.mult, ALU.add))
                own()
                step(dve.tensor_scalar(c(7), c(6), -ROUND_TO_256TH, None, ALU.add))
                own()
                step(dve.scalar_tensor_tensor(out=c(8), in0=c(7), scalar=-TWO_PI_A, in1=c(5), op0=ALU.mult, op1=ALU.add))
                own()
                step(dve.scalar_tensor_tensor(out=c(9), in0=c(7), scalar=-TWO_PI_B, in1=c(8), op0=ALU.mult, op1=ALU.add))
                own()
                step(dve.scalar_tensor_tensor(out=c(10), in0=c(7), scalar=-TWO_PI_C, in1=c(9), op0=ALU.mult, op1=ALU.add))
                own()
                step(dve.tensor_scalar(c(11), c(10), INV_TWO_PI, None, ALU.mult))

                def to_turns(t):
                    step(dve.tensor_scalar(turn_f[:, t], steps[:, t], c(7), None, ALU.mult))
                    own()
                    step(dve.tensor_scalar(turns_w[:, 0, t], turn_f[:, t], ROUND_TO_1, -ROUND_TO_1, ALU.add, ALU.add))
                    own()
                    step(dve.tensor_tensor(turn_c[:, t], turn_f[:, t], turns_w[:, 0, t], ALU.subtract))
                    own()
                    step(dve.scalar_tensor_tensor(out=turns[:, 0, t], in0=steps[:, t], scalar=c(11), in1=turn_c[:, t],
                                                  op0=ALU.mult, op1=ALU.add))
                    own()
                    step(dve.tensor_scalar(turns[:, 1, t], turns[:, 0, t], 0.25, None, ALU.add))
                    own()
                    step(dve.tensor_scalar(turns_w[:, :, t], turns[:, :, t], ROUND_TO_1, -ROUND_TO_1, ALU.add, ALU.add))
                    own()
                    dve.tensor_tensor(turns_r[:, :, t], turns[:, :, t], turns_w[:, :, t], ALU.subtract)\
                       .then_inc(turns_made, 1)

                to_turns(slice(1, 2))
                dve.wait_ge(mod_a_summed, 1)
                add_bias(0, NA, ps_h[:, 0, :])
                dve.tensor_scalar(scale_a[:, :, :], part(SCALE_A), 1.0, None, ALU.add).then_inc(mod_a_made, 1)
                step(dve.tensor_scalar(c(13), c(3), E_REST, 1.0, ALU.mult, ALU.add))
                step(dve.tensor_tensor(c(15), lam_re, lam_re, ALU.mult))
                own()
                dve.wait_ge(mag_raised, 1)
                step(dve.tensor_tensor(c(12), c(4), c(13), ALU.mult))
                step(dve.scalar_tensor_tensor(out=c(16), in0=lam_im, scalar=lam_im, in1=c(15), op0=ALU.mult, op1=ALU.add))
                own()
                step(dve.reciprocal(c(17), c(16)))
                dve.wait_ge(trig1_made, 1)
                step(dve.tensor_scalar(c(14), trig1[:, 0, :], c(12), None, ALU.mult))
                step(dve.tensor_scalar(c(18), trig1[:, 1, :], c(12), -1.0, ALU.mult, ALU.add))
                own()
                step(dve.tensor_tensor(c(19), c(14), lam_im, ALU.mult))
                step(dve.tensor_tensor(c(21), c(18), lam_im, ALU.mult))
                own()
                step(dve.scalar_tensor_tensor(out=c(22), in0=c(14), scalar=lam_re, in1=c(21), op0=ALU.mult,
                                              op1=ALU.subtract))
                step(dve.scalar_tensor_tensor(out=c(20), in0=c(18), scalar=lam_re, in1=c(19), op0=ALU.mult, op1=ALU.add))
                own()
                step(dve.tensor_scalar(c(23), c(22), c(17), sign[:, :], ALU.mult, ALU.mult))
                step(dve.tensor_tensor(c(24), c(20), c(17), ALU.mult))
                own()
                dve.wait_ge(bc_loaded, 16 * N_BC_LOADS)
                step(dve.tensor_scalar(b_tmp[:, :], b_second[:, :], c(23), None, ALU.mult))
                own()
                dve.scalar_tensor_tensor(out=b_bar[:, :], in0=b_first[:, :], scalar=c(24), in1=b_tmp[:, :],
                                         op0=ALU.mult, op1=ALU.subtract).then_inc(b_bar_made, 1)
                high_u(0)
                to_turns(slice(0, L))
                step(dve.tensor_scalar(decay[:, :], steps[:, :], 0.0, c(12), ALU.mult, ALU.add))
                own()
                dve.wait_ge(gate_a_summed, 1)
                add_bias(NA, NA + ND, ps_h[:, 1, :])
                dve.tensor_copy(carried[0][:, :], sign[:, :]).then_inc(gate_a_made, 1)

            def rest_of_mod():
                dve.wait_ge(vecs2_made, 1)
                dve.wait_ge(mod_summed, 1)
                add_bias(NA + ND, NM + NCC, ps_ff[:, 0, :])
                dve.tensor_copy(carried[1][:, :], sign[:, :]).then_inc(mod_rest_made, 1)

            def fill():
                set_up()
                dve.wait_ge(x_loaded[1], 16)
                stats_of_x(1)
                dve.wait_ge(trig_made, 2)
                rotate_and_scan(0)
                make_state(0)
                rest_of_mod()
                add_skip(0, [0])
                normalise_x(1)
                add_skip(0, [1])
                add_gated(0)
                normalise_y1(0, range(TS))
                normalise_y1(0, range(TS, NT))
                make_v(0, None, (0, 1))
                dve.wait_ge(mod_made, MOD_STEPS)
                rotate_and_scan(1, [0])
                dve.wait_ge(x_loaded[2], 16)
                stats_of_x(2)
                rotate_and_scan(1, [1])
                make_state(1)
                add_skip(1)
                normalise_x(2)
                add_gated(1)
                high_u(2)
                normalise_y1(1)
                dve.wait_ge(x_loaded[3], 16 * (NG - 3))
                stats_of_x(3)
                make_v(1, NF, (0, 1))
                rotate_and_scan(2)
                make_state(2)

            def tick(k):
                a, b, c = k, k - 1, k - 2
                if not has(k, 2):
                    gate_last_ff(c - 1)
                add_ff(c - 1)
                if has(k, 1):
                    add_skip(b)
                if has(k, 0):
                    normalise_x(a)
                if has(k, 0):
                    high_u(a)
                if has(k, 1):
                    add_gated(b)
                if has(k, 0):
                    rotate_and_scan(a)
                if has(k, 1):
                    normalise_y1(b)
                if has(k, 0):
                    make_state(a)
                if has(k, 1):
                    make_v(b, c * NF + NF, (1, 0))
                if has(k, -1):
                    stats_of_x(k + 1)

            run(dve, fill, tick, NG + 2)

        @block.scalar
        def _(act):
            def gelu(c, f):
                i = c * NF + f
                act.wait_ge(f1_done, i + 1)
                if not (isinstance(c, int) and i < HS):
                    act.wait_ge(h_low, i + 1 - HS)
                    act.wait_ge(f2_done, i + 1 - HS)
                act.activation(h[:, f % HS, :], ps_h[:, f % 2, :], ACT.Gelu_apprx_tanh, bias=vec(V_B1 + f))\
                   .then_inc(h_made, 1)
                act.activation(hh[:, f % HS, :], ps_h[:, f % 2, :], ACT.Gelu_apprx_tanh, bias=vec(V_B1 + f))\
                   .then_inc(h_high, 1)

            def swap_halves(dst, src, done):
                act.activation(dst[HIGH, :], src[LOW, :], ACT.Copy).then_inc(done, 1)
                act.activation(dst[LOW, :], src[HIGH, :], ACT.Copy).then_inc(done, 1)

            def swap_drive(g, ns=range(SEQ)):
                for n in ns:
                    act.wait_ge(bu_summed, g * SEQ + n + 1)
                    swap_halves(seq(bu_sw, n), bank(ps_p, n, 0), bu_swapped)

            def swap_scanned(g, ns=range(SEQ)):
                for n in ns:
                    act.wait_ge(scanned, g * SEQ + n + 1)
                    swap_halves(seq(z_sw, n), seq(z, n), z_swapped)

            def make_u(g):
                for n in range(SEQ):
                    act.wait_ge(xn_turned, g * SEQ + n + 1)
                    for d in range(ND):
                        act.activation(seq(u[:, d], n), bank(ps_p, n, d), ACT.Identity,
                                       scale=at_batch(scale_a, d, g, n),
                                       bias=at_batch(mod, SHIFT_A + d, g, n)).then_inc(u_made, 1)

            def make_u_and_high(g):
                for n in range(SEQ):
                    act.wait_ge(xn_turned, g * SEQ + n + 1)
                    for tile, made in ((u, u_made), (uh, u_high_early)):
                        for d in range(ND):
                            act.activation(seq(tile[:, d], n), bank(ps_p, n, d), ACT.Identity,
                                           scale=at_batch(scale_a, d, g, n),
                                           bias=at_batch(mod, SHIFT_A + d, g, n)).then_inc(made, 1)

            def gate_a(g, n):
                for d in range(ND):
                    act.wait_ge(a_sum_made, (g * SEQ + n) * ND + d + 1)
                    act.activation(seq(a_gated[:, d], n), seq(a_sum[:, d], n), ACT.Copy,
                                   scale=at_batch(mod, GATE_A + d, g, n)).then_inc(a_gated_made, 1)

            def first_v(g):
                act.wait_ge(yn_turned, g * SEQ + 1)
                for d in range(ND):
                    act.activation(seq(v[:, d], 0), bank(ps_q, 0, d), ACT.Identity, scale=at_batch(scale_v, d, g, 0),
                                   bias=at_batch(shift_v, d, g, 0)).then_inc(v_made_act, 1)

            def gate_ff(g, tiles):
                act.wait_ge(f2_done, g * NF + NF)
                for n in range(SEQ):
                    for d in tiles:
                        act.activation(seq(ff[:, d], n), seq(ps_ff[:, d], n), ACT.Identity,
                                       scale=at_batch(mod, GATE_F + d, g, n),
                                       bias=at_batch(gate_b2, d, g, n)).then_inc(ff_made, 1)

            def high_weights(n):
                act.wait_ge(w_loaded[n], 16)
                full = w1[:, :, :].rearrange("p a b -> p (a b)") if n == 0 else h[:, :, :].rearrange("p a b -> p (a b)")
                high = (w1h, w2h)[n][:, :, :].rearrange("p a b -> p (a b)")
                for m in range(4):
                    act.activation(high[:, m * 512:(m + 1) * 512], full[:, m * 512:(m + 1) * 512], ACT.Copy)\
                       .then_inc(w_high, 1)

            def fill():
                act.preload_act_table(ACT.Sin)
                act.wait_ge(vec_consts, VEC_CONSTS)
                act.wait_ge(turns_made, 1)
                act.activation(trig1[:, :, :], turns_r[:, :, 1:2], ACT.Sin, scale=TWO_PI_BELOW).then_inc(trig1_made, 1)
                act.wait_ge(mod_a_made, 1)
                make_u(0)
                act.wait_ge(b_turned, 1)
                b_cols = ps_q[:, 0, 0:D].rearrange("p (k d) -> p k d", d=P)
                act.activation(bT[:, :, :], b_cols, ACT.Copy).then_inc(b_high, 1)
                act.activation(bTh[:, :, :], b_cols, ACT.Copy).then_inc(b_high, 1)
                act.wait_ge(c_turned, 1)
                c_cols = ps_q[:, 1, 0:D].rearrange("p (k d) -> p k d", d=P)
                act.activation(cT[:, :, :], c_cols, ACT.Copy, scale=twice_sign[:, :]).then_inc(c_high, 1)
                act.activation(cTh[:, :, :], c_cols, ACT.Copy, scale=twice_sign[:, :]).then_inc(c_high, 1)
                act.activation(vecs[:, NV1:], ps_q[:, 1, D:D + NV2], ACT.Copy).then_inc(vecs2_made, 1)
                act.wait_ge(vecs2_made, 1)
                act.wait_ge(turns_made, 2)
                act.activation(cos_t[:, :], turns_r[:, 1, :], ACT.Sin, scale=TWO_PI_BELOW).then_inc(trig_made, 1)
                act.activation(sin_t[:, :], turns_r[:, 0, :], ACT.Sin, scale=two_pi[:, :]).then_inc(trig_made, 1)
                swap_drive(0)
                high_weights(0)
                swap_scanned(0)
                high_weights(1)
                act.preload_act_table(ACT.Gelu_apprx_tanh)
                act.wait_ge(gate_a_made, 1)
                gate_a(0, 0)
                gate_a(0, 1)
                make_u_and_high(1)
                act.wait_ge(mod_made, MOD_STEPS)
                first_v(0)
                swap_drive(1, [0])
                act.wait_ge(w_low, 8)
                gelu(0, 0)
                swap_drive(1, [1])
                gelu(0, 1)
                swap_scanned(1)
                gelu(0, 2)
                gelu(0, 3)
                gate_a(1, 0)
                gate_a(1, 1)
                gelu(0, 4)
                make_u(2)
                gelu(0, 5)
                gelu(0, 6)
                first_v(1)
                gelu(0, 7)
                swap_drive(2)
                swap_scanned(2, [0])
                swap_scanned(2, [1])

            def tick(k):
                a, b, c = k, k - 1, k - 2
                gate_ff(c - 1, range(ND) if has(k, 2) else [0])
                if has(k, 2):
                    gelu(c, 0)
                    gelu(c, 1)
                if has(k, 1):
                    gate_a(b, 0)
                    gate_a(b, 1)
                if has(k, 2):
                    gelu(c, 2)
                if has(k, 0):
                    make_u(a)
                if has(k, 2):
                    gelu(c, 3)
                if has(k, 0):
                    swap_drive(a)
                if has(k, 2):
                    gelu(c, 4)
                    gelu(c, 5)
                if has(k, 0):
                    swap_scanned(a)
                if has(k, 2):
                    gelu(c, 6)
                if has(k, 2):
                    gelu(c, 7)
                if has(k, 1):
                    first_v(b)

            run(act, fill, tick, NG + 2)

        @block.tensor
        def _(pe):
            def split_product(dst, wh, wl, ah, al, start, stop):
                pe.matmul(dst, wl, ah, start=start, stop=False)
                pe.matmul(dst, wh, al, start=False, stop=False)
                return pe.matmul(dst, wh, ah, start=False, stop=stop)

            def f1(c, f, cols=slice(0, GT)):
                i = c * NF + f
                if f == 0:
                    pe.wait_ge(v_low, c * SEQ + cols.stop // L)
                if not (isinstance(c, int) and i < 2):
                    pe.wait_ge(h_high, i - 1)
                fs = slice(f * P, (f + 1) * P)
                for kt in range(ND):
                    last = split_product(ps_h[:, f % 2, cols], w1h[:, kt, fs], w1l[:, kt, fs], vh[:, kt, cols],
                                         vl[:, kt, cols], kt == 0, kt == ND - 1)
                if cols.stop == GT:
                    last.then_inc(f1_done, 1)

            def f2(c, f):
                pe.wait_ge(h_low, c * NF + f + 1)
                for d in range(ND):
                    cs = slice(d * P, (d + 1) * P)
                    last = split_product(ps_ff[:, d, :], w2h[:, f, cs], w2l[:, f, cs], hh[:, f % HS, :], hl[:, f % HS, :],
                                         f == 0, f == NF - 1)
                last.then_inc(f2_done, 1)

            def turn_to_columns(ps, n, src, done):
                for d in range(ND):
                    for j in range(TS):
                        last = pe.transpose(bank(ps, n, d)[:, j * P:(j + 1) * P], src[:, n * TS + j, d * P:(d + 1) * P],
                                            ident[:, :])
                last.then_inc(done, 1)

            def turn_to_rows(n, src, done):
                for j in range(TS):
                    for d in range(ND):
                        last = pe.transpose(ps_q[:, n, j * D + d * P:j * D + (d + 1) * P],
                                            src[:, d, (n * TS + j) * P:(n * TS + j + 1) * P], ident[:, :])
                last.then_inc(done, 1)

            def turn_x(g, first=False, ns=range(SEQ)):
                for n in ns:
                    pe.wait_ge(xn_made, g * NT + (n + 1) * TS)
                    if not first:
                        pe.wait_ge(a_sum_made, ((g - 1) * SEQ + n + 1) * ND)
                    turn_to_columns(ps_p, n, xn, xn_turned)

            def turn_gated(g, after_ff=True, ns=range(SEQ)):
                for n in ns:
                    pe.wait_ge(a_gated_made, (g * SEQ + n + 1) * ND)
                    if after_ff:
                        pe.wait_ge(out_made, (g - 2) * SEQ + n + 1)
                    turn_to_rows(n, a_gated, a_turned)

            def turn_y1(g):
                for n in range(SEQ):
                    pe.wait_ge(yn_made, g * NT + (n + 1) * TS)
                    turn_to_columns(ps_q, n, yn, yn_turned)

            def turn_ff(g, after_v):
                for n in range(SEQ):
                    if after_v:
                        pe.wait_ge(ff_made, (g * SEQ + n + 1) * ND)
                        pe.wait_ge(v_low, (g + 2) * SEQ)
                    else:
                        pe.wait_ge(ff_made, g * SEQ * ND + n + 1)
                        pe.wait_ge(last_ff_made, n + 1)
                        pe.wait_ge(out_made, (g - 1) * SEQ + n + 1)
                    turn_to_rows(n, ff, ff_turned)

            def sum_drive(g, ns=range(SEQ)):
                for n in ns:
                    pe.wait_ge(u_low, g * SEQ + n + 1)
                    for kt in range(ND):
                        last = split_product(bank(ps_p, n, 0), bTh[:, kt, :], bTl[:, kt, :], seq(uh[:, kt], n),
                                             seq(ul[:, kt], n), kt == 0, kt == ND - 1)
                    last.then_inc(bu_summed, 1)

            def sum_states(g):
                for n in range(SEQ):
                    pe.wait_ge(state_low, g * SEQ + n + 1)
                    for d in range(ND):
                        last = split_product(bank(ps_p, n, d), cTh[:, d, :], cTl[:, d, :], seq(state_h, n), seq(state_l, n),
                                             True, True)
                    last.then_inc(a_summed, 1)

            def modulate(tiles, ps, done):
                for ct in tiles:
                    w, m = (wm, ct) if ct < NM else (wc, ct - NM)
                    for kt in range(ND):
                        last = pe.matmul(ps[:, ct * NB:(ct + 1) * NB], w[:, kt, m * P:(m + 1) * P],
                                         t_cols[:, kt, :], start=(kt == 0), stop=(kt == ND - 1))
                if done is not None:
                    last.then_inc(done, 1)

            def fill():
                pe.wait_ge(pool_consts, POOL_CONSTS)
                pe.wait_ge(vecs_loaded, 16 * N_VEC_LOADS)
                pe.transpose(ps_p[:, 0, 0:NV1], vec_rows1[:, :], ident[0:NV1, 0:NV1])
                for d in range(ND):
                    last = pe.transpose(ps_p[:, 1, d * NB:(d + 1) * NB], t_rows[:, d * P:(d + 1) * P],
                                        ident[0:NB, 0:NB])
                last.then_inc(vecs_turned, 1)
                pe.wait_ge(wa_loaded, 16)
                pe.wait_ge(vecs_made, 2)
                modulate(range(NA), ps_h[:, 0, :], mod_a_summed)
                turn_x(0, first=True)
                pe.wait_ge(wb_loaded, 16)
                modulate(range(NA, NA + ND), ps_h[:, 1, :], gate_a_summed)
                pe.wait_ge(b_bar_made, 1)
                for d in range(ND):
                    last = pe.transpose(ps_q[:, 0, d * P:(d + 1) * P], b_bar[:, d * P:(d + 1) * P], ident[:, :])
                last.then_inc(b_turned, 1)
                pe.wait_ge(bc_loaded, 16 * N_BC_LOADS)
                pe.wait_ge(vecs2_loaded, 16 * 4)
                for d in range(ND):
                    pe.transpose(ps_q[:, 1, d * P:(d + 1) * P], c_rows[:, d, :], ident[:, :])
                pe.transpose(ps_q[:, 1, D:D + NV2], vec_rows2[:, :], ident[0:NV2, 0:NV2]).then_inc(c_turned, 1)
                pe.wait_ge(b_low, 1)
                sum_drive(0)
                modulate(range(NA + ND, 2 * NA), ps_ff[:, 0, :], None)
                pe.wait_ge(wm_loaded, 16)
                modulate(range(2 * NA, NM), ps_ff[:, 0, :], None)
                pe.wait_ge(wc_loaded, 16)
                modulate(range(NM, NM + NCC), ps_ff[:, 0, :], mod_summed)
                pe.wait_ge(c_low, 1)
                sum_states(0)
                for n in range(SEQ):
                    turn_gated(0, after_ff=False, ns=[n])
                    turn_x(1, ns=[n])
                turn_y1(0)
                sum_drive(1, [0])
                pe.wait_ge(w_low, 4)
                for n in range(SEQ):
                    for f in range(2):
                        f1(0, f, slice(n * L, (n + 1) * L))
                sum_drive(1, [1])
                f1(0, 2)
                pe.wait_ge(w_low, 8)
                pe.wait_ge(mod_made, MOD_STEPS)
                f2(0, 0)
                f1(0, 3)
                f2(0, 1)
                sum_states(1)
                f1(0, 4)
                turn_gated(1, after_ff=False)
                f2(0, 2)
                turn_x(2)
                f1(0, 5)
                f2(0, 3)
                f1(0, 6)
                turn_y1(1)
                f1(0, 7)
                sum_drive(2)
                f2(0, 4)
                f2(0, 5)
                f2(0, 6)
                f2(0, 7)
                f1(1, 0)
                f1(1, 1)

            def tick(k):
                a, b, c = k, k - 1, k - 2
                turn_ff(c - 1, after_v=has(k, 2))
                if has(k, 1):
                    sum_states(b)
                if has(k, 2):
                    f1(c, 2)
                    f2(c, 0)
                if has(k, 0):
                    turn_x(a)
                if has(k, 1):
                    turn_gated(b)
                if has(k, 2):
                    f1(c, 3)
                    f2(c, 1)
                if has(k, 0):
                    sum_drive(a)
                if has(k, 2):
                    f1(c, 4)
                    f2(c, 2)
                    f1(c, 5)
                    f2(c, 3)
                    f1(c, 6)
                    f2(c, 4)
                    f1(c, 7)
                if has(k, 1):
                    turn_y1(b)
                if has(k, 2):
                    f2(c, 5)
                    f2(c, 6)
                    f2(c, 7)
                if has(k, 1):
                    f1(b, 0)
                    f1(b, 1)

            run(pe, fill, tick, NG + 2)


_INS = ['x', 'cond_1024'] + ['L0_cond_' + n for n in (
    'Wm', 'bm', 'Lam_re', 'Lam_im', 'B_re', 'B_im', 'C_re', 'C_im', 'D_diag', 'log_step', 'Wc', 'bc', 'W1', 'b1', 'W2', 'b2')]


def kernel(**inputs):
    import numpy as np
    import concourse.bacc as bacc
    from concourse.bass_utils import run_bass_kernel_spmd

    nc = bacc.Bacc("TRN2", target_bir_lowering=False, num_devices=1)
    arrays, args = {}, []
    for name in _INS:
        a = np.ascontiguousarray(inputs[name])
        arrays["in_" + name] = a
        args.append(nc.dram_tensor("in_" + name, a.shape, mybir.dt.from_np(a.dtype), kind="ExternalInput").ap())
    shape = inputs["x"].shape
    args.append(nc.dram_tensor("out_y", shape, F32, kind="ExternalOutput").ap())
    cond_seq_kernel(nc, *args)
    r = run_bass_kernel_spmd(nc, [arrays], core_ids=[0])
    return r.results[0]["out_y"]
```
